# Optimizing a Trainium2 kernel written in Bass

```python
import numpy as np
import jax
import jax.numpy as jnp

def _softmax(x, axis=-1):
    return jax.nn.softmax(x, axis=axis)

def _gelu(x):
    return jax.nn.gelu(x, approximate=True)

def _silu(x):
    return jax.nn.silu(x)

def _sigmoid(x):
    return jax.nn.sigmoid(x)

def _layernorm(x, axis=-1, eps=1e-05):
    m = jnp.mean(x, axis=axis, keepdims=True)
    v = jnp.var(x, axis=axis, keepdims=True)
    return (x - m) / jnp.sqrt(v + eps)

def _scatter_add(tgt, idx, src, axis=0):
    return tgt.at[idx].add(src)

def _segment_sum(src, seg, n):
    return jax.ops.segment_sum(src, seg, n)
kernel_name = 'mk_gnn_resnorm_d1_gnn_r64_a435ef'

def setup_inputs(seed: int=0):
    np.random.seed(seed)
    _w = jnp.asarray

    def _rec_inputs():
        import jax
        import jax.numpy as jnp
        _gk = jax.random.key(seed)
        x = -0.000202 + 1 * jax.random.normal(jax.random.fold_in(_gk, 1), (100000, 128), jnp.float32)
        src = jax.random.randint(jax.random.fold_in(_gk, 2), (50000,), 0, 100000, jnp.int32)
        dst = jnp.minimum((100000 * jax.random.uniform(jax.random.fold_in(_gk, 3), (50000,)) ** 2.0).astype(jnp.int32), 99999)
        _o = jnp.argsort(dst, stable=True)
        src = src[_o]
        dst = dst[_o]
        edge_attr_16 = 0.00028786 + 0.999816 * jax.random.normal(jax.random.fold_in(_gk, 11), (50000, 16), jnp.float32)
        node_type_3 = jax.random.randint(jax.random.fold_in(_gk, 13), (100000,), 0, 3, jnp.int32)
        return (x, src, dst, edge_attr_16, node_type_3)
    x, src, dst, edge_attr_16, node_type_3 = _rec_inputs()

    def _L0_gnn_setup():
        import jax, jax.numpy as jnp
        import numpy as np
        N, E, C, ED = (50000, 9375, 128, 16)

        def _gat_params(key, c_in, c_out, edim):
            ks = jax.random.split(key, 6)
            s = lambda *sh: 1.0 / np.sqrt(sh[0])
            return dict(W=jax.random.normal(ks[0], (c_in, c_out), jnp.float32) * s(c_in), a_src=jax.random.normal(ks[1], (c_out,), jnp.float32) * s(c_out), a_dst=jax.random.normal(ks[2], (c_out,), jnp.float32) * s(c_out), We=jax.random.normal(ks[3], (edim, c_out), jnp.float32) * s(edim), a_edge=jax.random.normal(ks[4], (c_out,), jnp.float32) * s(c_out), b=jnp.zeros((c_out,), jnp.float32))

        def gat_conv(x, edge_index, edge_attr, W, a_src, a_dst, We, a_edge, b):
            src, dst = (edge_index[0], edge_index[1])
            n = x.shape[0]
            xs = x @ W
            al_s = xs @ a_src
            al_d = xs @ a_dst
            al_e = edge_attr @ We @ a_edge
            a = al_s[src] + al_d[dst] + al_e
            a = jnp.where(a > 0, a, 0.2 * a)
            m = jax.ops.segment_max(a, dst, num_segments=n)
            e = jnp.exp(a - m[dst])
            s = jax.ops.segment_sum(e, dst, num_segments=n)
            w = e / (s[dst] + 1e-16)
            out = jax.ops.segment_sum(w[:, None] * xs[src], dst, num_segments=n)
            return out + x + b
        key = jax.random.key(seed)
        k = jax.random.split(key, 8)
        inp = {'h': jax.random.normal(k[0], (N, C), jnp.float32), 'edge_index': jax.random.randint(k[1], (2, E), 0, N, jnp.int64), 'edge_attr': jax.random.normal(k[2], (E, ED), jnp.float32), 'node_type': jax.random.randint(k[3], (N,), 0, 3, jnp.int64)}
        for name, kk in (('v', k[4]), ('r', k[5]), ('i', k[6])):
            p = _gat_params(kk, C, C, ED)
            inp['W' + name] = p['W']
            inp['as' + name] = p['a_src']
            inp['ad' + name] = p['a_dst']
            inp['We' + name] = p['We']
            inp['ae' + name] = p['a_edge']
            inp['b' + name] = p['b']
        return inp
    _L0_gnn_all = _L0_gnn_setup()
    _L0_gnn_in = {k: v for k, v in _L0_gnn_all.items() if k in ('Wv', 'asv', 'adv', 'Wev', 'aev', 'bv', 'Wr', 'asr', 'adr', 'Wer', 'aer', 'br', 'Wi', 'asi', 'adi', 'Wei', 'aei', 'bi')}
    del _L0_gnn_all
    return {'x': x, 'src': src, 'dst': dst, 'edge_attr_16': edge_attr_16, 'node_type_3': node_type_3, 'L0_gnn_Wv': _L0_gnn_in['Wv'], 'L0_gnn_asv': _L0_gnn_in['asv'], 'L0_gnn_adv': _L0_gnn_in['adv'], 'L0_gnn_Wev': _L0_gnn_in['Wev'], 'L0_gnn_aev': _L0_gnn_in['aev'], 'L0_gnn_bv': _L0_gnn_in['bv'], 'L0_gnn_Wr': _L0_gnn_in['Wr'], 'L0_gnn_asr': _L0_gnn_in['asr'], 'L0_gnn_adr': _L0_gnn_in['adr'], 'L0_gnn_Wer': _L0_gnn_in['Wer'], 'L0_gnn_aer': _L0_gnn_in['aer'], 'L0_gnn_br': _L0_gnn_in['br'], 'L0_gnn_Wi': _L0_gnn_in['Wi'], 'L0_gnn_asi': _L0_gnn_in['asi'], 'L0_gnn_adi': _L0_gnn_in['adi'], 'L0_gnn_Wei': _L0_gnn_in['Wei'], 'L0_gnn_aei': _L0_gnn_in['aei'], 'L0_gnn_bi': _L0_gnn_in['bi']}

def reference(x, src, dst, edge_attr_16, node_type_3, L0_gnn_Wv, L0_gnn_asv, L0_gnn_adv, L0_gnn_Wev, L0_gnn_aev, L0_gnn_bv, L0_gnn_Wr, L0_gnn_asr, L0_gnn_adr, L0_gnn_Wer, L0_gnn_aer, L0_gnn_br, L0_gnn_Wi, L0_gnn_asi, L0_gnn_adi, L0_gnn_Wei, L0_gnn_aei, L0_gnn_bi):
    import jax
    import jax.numpy as jnp

    def _L0_gnn_ref(h, edge_index, edge_attr, node_type, Wv, asv, adv, Wev, aev, bv, Wr, asr, adr, Wer, aer, br, Wi, asi, adi, Wei, aei, bi):
        import jax, jax.numpy as jnp
        import numpy as np
        N, E, C, ED = (50000, 9375, 128, 16)

        def _gat_params(key, c_in, c_out, edim):
            ks = jax.random.split(key, 6)
            s = lambda *sh: 1.0 / np.sqrt(sh[0])
            return dict(W=jax.random.normal(ks[0], (c_in, c_out), jnp.float32) * s(c_in), a_src=jax.random.normal(ks[1], (c_out,), jnp.float32) * s(c_out), a_dst=jax.random.normal(ks[2], (c_out,), jnp.float32) * s(c_out), We=jax.random.normal(ks[3], (edim, c_out), jnp.float32) * s(edim), a_edge=jax.random.normal(ks[4], (c_out,), jnp.float32) * s(c_out), b=jnp.zeros((c_out,), jnp.float32))

        def gat_conv(x, edge_index, edge_attr, W, a_src, a_dst, We, a_edge, b):
            src, dst = (edge_index[0], edge_index[1])
            n = x.shape[0]
            xs = x @ W
            al_s = xs @ a_src
            al_d = xs @ a_dst
            al_e = edge_attr @ We @ a_edge
            a = al_s[src] + al_d[dst] + al_e
            a = jnp.where(a > 0, a, 0.2 * a)
            m = jax.ops.segment_max(a, dst, num_segments=n)
            e = jnp.exp(a - m[dst])
            s = jax.ops.segment_sum(e, dst, num_segments=n)
            w = e / (s[dst] + 1e-16)
            out = jax.ops.segment_sum(w[:, None] * xs[src], dst, num_segments=n)
            return out + x + b
        ov = gat_conv(h, edge_index, edge_attr, Wv, asv, adv, Wev, aev, bv)
        orr = gat_conv(h, edge_index, edge_attr, Wr, asr, adr, Wer, aer, br)
        oi = gat_conv(h, edge_index, edge_attr, Wi, asi, adi, Wei, aei, bi)
        is_var = (node_type == 0)[:, None]
        is_red = (node_type == 1)[:, None]
        out = jnp.where(is_var, ov, jnp.where(is_red, orr, oi))
        return jax.nn.relu(out)
    edge_index = jnp.stack([src, dst])
    x = _layernorm(x + _L0_gnn_ref(x, edge_index, edge_attr_16, node_type_3, L0_gnn_Wv, L0_gnn_asv, L0_gnn_adv, L0_gnn_Wev, L0_gnn_aev, L0_gnn_bv, L0_gnn_Wr, L0_gnn_asr, L0_gnn_adr, L0_gnn_Wer, L0_gnn_aer, L0_gnn_br, L0_gnn_Wi, L0_gnn_asi, L0_gnn_adi, L0_gnn_Wei, L0_gnn_aei, L0_gnn_bi), axis=-1)
    return x

_drawn_inputs = setup_inputs


def setup_inputs(seed=0):
    import zlib

    import numpy as np

    out = dict(_drawn_inputs(seed))
    spreads = {'L0_gnn_bv': (0.0, 0.313), 'L0_gnn_br': (0.0, 0.287), 'L0_gnn_bi': (0.0, 0.319)}
    factors = {'L0_gnn_asv': 8.577,
     'L0_gnn_adv': 64.0,
     'L0_gnn_Wev': 3.282,
     'L0_gnn_aev': 3.499,
     'L0_gnn_asr': 2.887,
     'L0_gnn_adr': 42.893,
     'L0_gnn_aer': 2.959,
     'L0_gnn_asi': 9.255,
     'L0_gnn_adi': 64.0,
     'L0_gnn_Wei': 3.73,
     'L0_gnn_aei': 3.653}
    for name, (base, spread) in spreads.items():
        noise = np.random.default_rng([zlib.crc32(name.encode()), seed]).standard_normal(out[name].shape)
        drawn = base * np.exp(spread * noise) if base else spread * noise
        out[name] = jnp.asarray(drawn.astype(out[name].dtype))
    for name, factor in factors.items():
        out[name] = (out[name] * factor).astype(out[name].dtype)
    return out
```

```python
import concourse.bass as bass
from concourse import mybir
from contextlib import ExitStack


def gat_kernel(nc, x, src, dst, edge_attr, node_type, convs, out):
    fp32 = mybir.dt.float32
    i32 = mybir.dt.int32
    ALU = mybir.AluOpType
    ACT = mybir.ActivationFunctionType
    X_AXIS = mybir.AxisListType.X

    N, C = x.shape
    E, ED = edge_attr.shape
    P = 128
    T = 3
    BIG = 1.0e30
    EPS = 1e-5
    TINY = 1e-16

    BJ = 8
    BLOCK = P * BJ
    FULL_BLOCKS = N // BLOCK
    TAIL_P = (N - FULL_BLOCKS * BLOCK) // BJ
    BLOCKS = FULL_BLOCKS + 1
    assert FULL_BLOCKS * BLOCK + TAIL_P * BJ == N
    SLOTS = 4
    BLOCK_LOOPS = FULL_BLOCKS // SLOTS

    U = 7
    LANE_EDGES = -(-E // (P * U * SLOTS)) * U * SLOTS
    GROUPS = LANE_EDGES // U
    FULL_LANES = E // LANE_EDGES
    LAST_LANE = E - FULL_LANES * LANE_EDGES
    assert FULL_LANES == P - 1 and 1 < LAST_LANE < LANE_EDGES
    PAD_DST = 1 << 17
    SKIP = 1 << 18
    assert N < PAD_DST
    RING = GROUPS // 2
    ROW = C + 1 + T
    ATTR_CHUNK = LANE_EDGES // 4

    def back(count, n):
        return max(count - n, 0) if isinstance(count, int) else count - n

    node_rows = nc.dram_tensor("node_rows", (N, ROW), fp32).ap()

    def first_rows(t, n, p):
        return t[bass.ds(n, p * BJ), :].rearrange("(p j) c -> p j c", j=BJ)

    with ExitStack() as ctx:
        def sb(name, shape, dt=fp32):
            return ctx.enter_context(nc.sbuf_tensor(name, shape, dt))

        def pb(name):
            return ctx.enter_context(nc.psum_tensor(name, [P, 512], fp32))

        def sem(name):
            return ctx.enter_context(nc.semaphore(name))

        ident = sb("ident", [P, P])
        ones = sb("ones", [P, P])
        W3 = sb("W3", [P, T, C])
        WT = sb("WT", [P, T, C])
        We3 = sb("We3", [ED, T, C])
        WeT = sb("WeT", [P, T, ED])
        a_src = sb("a_src", [P, T])
        a_dst = sb("a_dst", [P, T])
        a_edge = sb("a_edge", [P, T])
        a_edge_bc = sb("a_edge_bc", [P, T, P])
        V_src = sb("V_src", [P, T])
        V_dst = sb("V_dst", [P, T])
        g_edge = sb("g_edge", [P, T, ED])
        bias_diag = sb("bias_diag", [BJ * T, BJ * C])
        types = sb("types", [P, BLOCKS, BJ], i32)
        src_idx = sb("src_idx", [P, LANE_EDGES], i32)
        row_idx = sb("row_idx", [P, LANE_EDGES], i32)
        out_idx = sb("out_idx", [P, LANE_EDGES], i32)
        fix_idx = sb("fix_idx", [P, 1], i32)
        restart = sb("restart", [P, LANE_EDGES])
        head_end = sb("head_end", [P, LANE_EDGES])
        edge_score = sb("edge_score", [P, LANE_EDGES, T])
        M_all = sb("M_all", [P, LANE_EDGES + 1])
        S_all = sb("S_all", [P, LANE_EDGES + 1])
        xs_ring = sb("xs_ring", [P, RING, U * C])
        rows = sb("rows", [P, SLOTS, BJ, ROW])
        obuf = sb("obuf", [P, SLOTS, BJ, C])
        z = sb("z", [P, 2, BJ, C])
        xT = sb("xT", [P, 2, BJ * C])
        onehotT = sb("onehotT", [BJ * T, 2, P])
        xst = sb("xst", [P, 2, U, C])
        px = sb("px", [P, U, C])
        acc = sb("acc", [P, 2, U, C])
        accT = sb("accT", [P, U * C])
        head_acc = sb("head_acc", [P, C])
        onehot = sb("onehot", [P, 2, BJ, T])
        types1h = sb("types1h", [P, BJ])
        prod = sb("prod", [P, BJ, T])
        score = sb("score", [P, 2, BJ])
        expo = sb("expo", [P, 2, 2, U])
        fp = sb("fp", [P, 2, 2, U])
        rs = sb("rs", [P, BJ])
        kk = sb("kk", [P, 2, U, T])
        stats = sb("stats", [P, 2, BJ, 6])
        st = sb("st", [P, 2, 5, BJ])
        std = sb("std", [P, 2, BJ])
        rstd = sb("rstd", [P, 2, BJ])
        nbias = sb("nbias", [P, 2, BJ])
        eps = sb("eps", [P, 1])
        cols = sb("cols", [P, 6])
        cin = sb("cin", [P, 4])

        dI = acc[:, 0, 0:4, :].rearrange("p a c -> p (a c)")[:, 0:LANE_EDGES].bitcast(i32)
        nI = acc[:, 1, 0:4, :].rearrange("p a c -> p (a c)")[:, 0:LANE_EDGES].bitcast(i32)
        pI = xst[:, 0, 0:4, :].rearrange("p a c -> p (a c)")[:, 0:LANE_EDGES].bitcast(i32)
        dF = xst[:, 1, 0:4, :].rearrange("p a c -> p (a c)")[:, 0:LANE_EDGES]
        nF = accT[:, 0:LANE_EDGES]
        pF = accT[:, 448:448 + LANE_EDGES]
        hd = px[:, 0:4, :].rearrange("p a c -> p (a c)")[:, 0:LANE_EDGES]
        attr_buf = xs_ring[:, RING - 4:RING, :].rearrange("p a b -> p (a b)")
        attr_c = [attr_buf[:, h * ATTR_CHUNK * ED:(h + 1) * ATTR_CHUNK * ED]
                  .rearrange("p (j d) -> p j d", d=ED) for h in range(2)]
        attr_prod = xs_ring[:, RING - 6:RING - 4, :].rearrange("p a b -> p (a b)")[:, 0:ATTR_CHUNK * ED]\
            .rearrange("p (j d) -> p j d", d=ED)

        ps_x = [pb("ps_x0"), pb("ps_x1")]
        ps_b = [pb("ps_b0"), pb("ps_b1")]
        ps_w = [pb("ps_w0"), pb("ps_w1")]
        ps_a = pb("ps_a")
        ps_o = pb("ps_o")

        s_const = sem("s_const")
        s_par = sem("s_par")
        s_bias = sem("s_bias")
        s_pad = sem("s_pad")
        s_src = sem("s_src")
        s_dst = sem("s_dst")
        s_types = sem("s_types")
        s_attr = [sem(f"s_attr{h}") for h in range(2)]
        s_attr_used = sem("s_attr_used")
        s_setT = sem("s_setT")
        s_setC = sem("s_setC")
        s_idx = sem("s_idx")
        s_row_in = [sem(f"s_row_in{k}") for k in range(SLOTS)]
        s_row_out = [sem(f"s_row_out{k}") for k in range(SLOTS)]
        s_out = [sem(f"s_out{k}") for k in range(SLOTS)]
        s_onehot = sem("s_onehot")
        s_row_oh = sem("s_row_oh")
        s_rows_full = sem("s_rows_full")
        s_xT_ps = sem("s_xT_ps")
        s_xT = sem("s_xT")
        s_al = sem("s_al")
        s_al_used = sem("s_al_used")
        s_ohT_ps = sem("s_ohT_ps")
        s_ohT = sem("s_ohT")
        s_bsel = sem("s_bsel")
        s_bsel_used = sem("s_bsel_used")
        s_z = sem("s_z")
        s_var = sem("s_var")
        s_std = sem("s_std")
        s_norm_par = sem("s_norm_par")
        s_norm = sem("s_norm")
        s_gx = [sem(f"s_gx{k}") for k in range(SLOTS)]
        s_gr = [sem(f"s_gr{k}") for k in range(SLOTS)]
        s_sc = [sem(f"s_sc{k}") for k in range(SLOTS)]
        s_xs = sem("s_xs")
        s_staged = sem("s_staged")
        e_xT_ps = sem("e_xT_ps")
        e_xT = sem("e_xT")
        e_al = sem("e_al")
        e_al_used = sem("e_al_used")
        e_oh = sem("e_oh")
        e_ohT_ps = sem("e_ohT_ps")
        e_ohT = sem("e_ohT")
        e_expo = sem("e_expo")
        e_exp = sem("e_exp")
        e_px = sem("e_px")
        e_acc = sem("e_acc")
        e_accT_ps = sem("e_accT_ps")
        e_accT = sem("e_accT")
        e_w = sem("e_w")
        e_w_used = sem("e_w_used")
        e_bsel = sem("e_bsel")
        e_bsel_used = sem("e_bsel_used")
        e_z = sem("e_z")
        e_var = sem("e_var")
        e_std = sem("e_std")
        e_norm_par = sem("e_norm_par")
        e_norm = sem("e_norm")
        s_dve_setup = sem("s_dve_setup")
        s_node_oh = sem("s_node_oh")
        s_node_st = sem("s_node_st")
        s_node_np = sem("s_node_np")
        e_dve_a = sem("e_dve_a")
        e_dve_b = sem("e_dve_b")
        e_dve_c = sem("e_dve_c")
        e_dve_n = sem("e_dve_n")
        e_head = sem("e_head")
        s_dve_last = sem("s_dve_last")
        f_pe = sem("f_pe")
        f_dve = sem("f_dve")
        f_act = sem("f_act")
        f_rows = sem("f_rows")
        f_out = sem("f_out")

        PAR_LOADS = 5 * T
        BIAS_LOADS = BJ * T

        block = ctx.enter_context(nc.Block())

        @block.sync
        def _(sp):
            def value(v):
                return v if isinstance(v, int) else sp.snap(sp.to_reg(v))

            def load_block(b, k, p, waits):
                n = value(b * BLOCK)
                waits = waits and [value(v) for v in waits]
                if waits:
                    sp.wait_ge(s_row_out[k], waits[0])
                    sp.wait_ge(s_z, waits[1])
                sp.dma_start(rows[0:p, k, :, 0:C], first_rows(x, n, p)).then_inc(s_row_in[k], 16)

            def store_block(b, k, p):
                n, done = value(b * BLOCK), value(b + 1)
                sp.wait_ge(s_rows_full, done)
                sp.wait_ge(s_row_oh, done)
                sp.dma_start(first_rows(node_rows, n, p), rows[0:p, k, :, :]).then_inc(s_row_out[k], 16)
                sp.wait_ge(s_norm, done)
                sp.dma_start(first_rows(out, n, p), obuf[0:p, k, :, :]).then_inc(s_out[k], 16)

            sp.wait_ge(s_pad, 1)
            flat = src[0:FULL_LANES * LANE_EDGES].rearrange("(p j) -> p j", j=LANE_EDGES)
            sp.dma_start(src_idx[0:112, :], flat[0:112, :]).then_inc(s_src, 16)
            sp.dma_start(src_idx[112:FULL_LANES, :], flat[112:FULL_LANES, :]).then_inc(s_src, 16)
            sp.dma_start(src_idx[FULL_LANES:P, 0:LAST_LANE],
                         src[FULL_LANES * LANE_EDGES:E].rearrange("(a j) -> a j", a=1)).then_inc(s_src, 16)
            for t, (W, a_s, a_d, We, a_e, b) in enumerate(convs):
                sp.dma_start(W3[:, t, :], W).then_inc(s_par, 16)
                sp.dma_start(We3[:, t, :], We).then_inc(s_par, 16)
                for col, a in ((a_src, a_s), (a_dst, a_d), (a_edge, a_e)):
                    sp.dma_start(col[:, t:t + 1], a.rearrange("(c a) -> c a", a=1)).then_inc(s_par, 16)
            for b in range(SLOTS - 1):
                load_block(b, b, P, None)
            sp.wait_ge(s_pad, 3)
            sp.dma_start(types[:, 0:FULL_BLOCKS, :],
                         node_type[0:FULL_BLOCKS * BLOCK].rearrange("(b p j) -> p b j", p=P, j=BJ))\
                .then_inc(s_types, 16)
            sp.dma_start(types[0:TAIL_P, FULL_BLOCKS, :],
                         node_type[FULL_BLOCKS * BLOCK:N].rearrange("(p j) -> p j", j=BJ)).then_inc(s_types, 16)
            for t, conv in enumerate(convs):
                for j in range(BJ):
                    sp.dma_start(bias_diag[j * T + t:j * T + t + 1, j * C:(j + 1) * C],
                                 conv[5].rearrange("(a c) -> a c", a=1)).then_inc(s_bias, 16)

            def attr_load(c):
                h = c % 2
                lo, hi = c * ATTR_CHUNK, (c + 1) * ATTR_CHUNK
                full = edge_attr[0:FULL_LANES * LANE_EDGES, :].rearrange("(p j) d -> p j d", j=LANE_EDGES)
                sp.dma_start(attr_c[h][0:112], full[0:112, lo:hi, :]).then_inc(s_attr[h], 16)
                sp.dma_start(attr_c[h][112:FULL_LANES], full[112:FULL_LANES, lo:hi, :]).then_inc(s_attr[h], 16)
                n = min(hi, LAST_LANE) - lo
                if n > 0:
                    e = FULL_LANES * LANE_EDGES + lo
                    sp.dma_start(attr_c[h][FULL_LANES:P, 0:n, :],
                                 edge_attr[e:e + n, :].rearrange("(a j) d -> a j d", a=1)).then_inc(s_attr[h], 16)

            sp.wait_ge(s_pad, 8)
            attr_load(0)
            attr_load(1)
            first = FULL_LANES * LANE_EDGES
            for buf, shift in ((dI, 0), (nI, 1), (pI, -1)):
                body = dst[max(shift, 0):][0:FULL_LANES * LANE_EDGES].rearrange("(p j) -> p j", j=LANE_EDGES)
                if shift >= 0:
                    sp.dma_start(buf[0:112, :], body[0:112, :]).then_inc(s_dst, 16)
                    sp.dma_start(buf[112:FULL_LANES, :], body[112:FULL_LANES, :]).then_inc(s_dst, 16)
                else:
                    sp.dma_start(buf[0:1, 1:LANE_EDGES],
                                 dst[0:LANE_EDGES - 1].rearrange("(a j) -> a j", a=1)).then_inc(s_dst, 16)
                    body = dst[LANE_EDGES - 1:first - 1].rearrange("(p j) -> p j", j=LANE_EDGES)
                    sp.dma_start(buf[1:FULL_LANES, :], body).then_inc(s_dst, 16)
                n = min(E, E - shift) - first if shift >= 0 else LAST_LANE + 1
                sp.dma_start(buf[FULL_LANES:P, 0:n],
                             dst[first + shift:first + shift + n].rearrange("(a j) -> a j", a=1))\
                    .then_inc(s_dst, 16)
            sp.wait_ge(s_attr_used, 1)
            attr_load(2)
            sp.wait_ge(s_attr_used, 2)
            attr_load(3)

            def step(b, i, k):
                ahead = b + SLOTS - 1
                ka = (k + SLOTS - 1) % SLOTS
                if k > 0 or not isinstance(b, int) or b > 0:
                    load_block(ahead, ka, P, (16 * (i + (0 if k == 0 else 1)), b))
                store_block(b, k, P)

            load_block(SLOTS - 1, SLOTS - 1, P, None)
            store_block(0, 0, P)
            for k in range(1, SLOTS):
                step(k, 0, k)
            with sp.Fori(1, BLOCK_LOOPS - 1) as i:
                for k in range(SLOTS):
                    step(SLOTS * i + k, i, k)
            for b in range(SLOTS * (BLOCK_LOOPS - 1), BLOCKS):
                k = b % SLOTS
                ahead = b + SLOTS - 1
                if ahead < BLOCKS:
                    load_block(ahead, ahead % SLOTS, P if ahead < FULL_BLOCKS else TAIL_P,
                               (16 * ((b - 1) // SLOTS + 1), b))
                store_block(b, k, P if b < FULL_BLOCKS else TAIL_P)

        @block.gpsimd
        def _(pool):
            pool.memset(src_idx[:, :], 0).then_inc(s_pad, 1)
            pool.memset(ident[:, :], 0.0).then_inc(s_const, 1)
            pool.memset(types[:, :, :], 0).then_inc(s_pad, 1)
            pool.memset(bias_diag[:, :], 0.0).then_inc(s_pad, 1)
            pool.wait_ge(s_const, 1)
            pool.affine_select(out=ident[:, :], in_=ident[:, :], compare_op=ALU.not_equal, fill=1.0,
                               base=0, pattern=[[-1, P]], channel_multiplier=1).then_inc(s_const, 1)
            pool.memset(ones[:, :], 1.0).then_inc(s_const, 1)
            for buf in (attr_c[0], attr_c[1]):
                pool.memset(buf, 0.0).then_inc(s_pad, 1)
            for buf in (dI, nI, pI):
                pool.memset(buf, PAD_DST).then_inc(s_pad, 1)

            def gather(idx, j, into, table, done):
                pool.indirect_dma_start(out=into, out_offset=None, in_=table, in_offset=bass.IndirectOffsetOnAxis(
                    ap=idx[:, j:j + 1], axis=0)).then_inc(done, 16)

            def gather_src(g):
                if g >= RING:
                    pool.wait_ge(s_staged, g - RING + 1)
                for u in range(U):
                    gather(src_idx, g * U + u, xs_ring[:, g % RING, u * C:(u + 1) * C], x, s_gx[g % SLOTS])

            def announce_src(g):
                pool.wait_ge(s_gx[g % SLOTS], 16 * U * (g // SLOTS + 1))
                pool.sem_inc(s_xs, 1)

            def gather_rows(g):
                if g >= SLOTS:
                    pool.wait_ge(e_z, g - SLOTS + 1)
                for u in range(U):
                    gather(row_idx, g * U + u, rows[:, g % SLOTS, u, :], node_rows, s_gr[g % SLOTS])

            def scatter_out(g):
                pool.wait_ge(e_norm, g + 1)
                for u in range(U):
                    j = g * U + u
                    pool.indirect_dma_start(
                        out=out, out_offset=bass.IndirectOffsetOnAxis(ap=out_idx[:, j:j + 1], axis=0),
                        in_=obuf[:, g % SLOTS, u, :], in_offset=None,
                        bounds_check=N - 1, oob_is_err=False).then_inc(s_sc[g % SLOTS], 16)

            pool.wait_ge(s_src, 48)
            for g in range(RING):
                if g == RING - 6:
                    pool.wait_ge(s_attr_used, 4)
                gather_src(g)
                if g >= 2:
                    announce_src(g - 2)
            for k in range(SLOTS):
                pool.wait_ge(s_row_out[k], 16 * ((BLOCKS - 1 - k) // SLOTS + 1))
                pool.wait_ge(s_out[k], 16 * ((BLOCKS - 1 - k) // SLOTS + 1))
            pool.wait_ge(s_z, BLOCKS)
            pool.wait_ge(s_idx, 1)
            for g in range(GROUPS + 3):
                if g < GROUPS:
                    gather_rows(g)
                if RING - 2 <= g + RING - 2 < GROUPS:
                    announce_src(g + RING - 2)
                if g + RING < GROUPS:
                    gather_src(g + RING)
                if g >= 3:
                    scatter_out(g - 3)
            pool.wait_ge(e_z, GROUPS)
            gather(row_idx, 0, rows[:, 0, 0, :], node_rows, f_rows)
            for k in range(SLOTS):
                pool.wait_ge(s_sc[k], 16 * U * (GROUPS // SLOTS))
            pool.wait_ge(f_act, 4)
            pool.indirect_dma_start(
                out=out, out_offset=bass.IndirectOffsetOnAxis(ap=fix_idx[:, 0:1], axis=0),
                in_=obuf[:, 0, 0, :], in_offset=None, bounds_check=N - 1, oob_is_err=False).then_inc(f_out, 16)
            pool.wait_ge(f_out, 16)

        @block.tensor
        def _(pe):
            def transpose(o, i, n):
                return nc.tensor.transpose(o, i, ident[0:n, 0:n])

            pe.wait_ge(s_const, 3)
            pe.wait_ge(s_par, 16 * PAR_LOADS)
            for t in range(T):
                transpose(ps_x[0][:, t * C:(t + 1) * C], W3[:, t, :], P)
            for t in range(T):
                last = transpose(ps_x[1][:, t * ED:(t + 1) * ED], We3[:, t, :], ED)
            last.then_inc(s_setT, 1)
            pe.wait_ge(s_setC, 1)
            for t in range(T):
                nc.tensor.matmul(ps_a[:, t:t + 1], lhsT=WT[:, t, :], rhs=a_src[:, t:t + 1], start=True, stop=True)
                nc.tensor.matmul(ps_a[:, T + t:T + t + 1], lhsT=WT[:, t, :], rhs=a_dst[:, t:t + 1],
                                 start=True, stop=True)
                last = nc.tensor.matmul(ps_a[:, 64 + t * ED:64 + (t + 1) * ED], lhsT=a_edge_bc[:, t, :],
                                        rhs=WeT[:, t, :], start=True, stop=True)
            last.then_inc(s_setT, 1)
            pe.wait_ge(s_setC, 2)

            pe.wait_ge(s_bias, 16 * BIAS_LOADS)

            def node_block(b, i, k, p):
                q = k % 2
                pe.wait_ge(s_row_in[k], 16 * (i + 1))
                pe.wait_ge(s_xT, 2 * b)
                for h in range(2):
                    for j in range(4 * h, 4 * h + 4):
                        last = transpose(ps_x[h][:, (j % 4) * P:(j % 4) * P + p], rows[0:p, k, j, 0:C], p)
                    last.then_inc(s_xT_ps, 1)
                pe.wait_ge(s_onehot, b + 1)
                pe.wait_ge(s_ohT, b)
                transpose(ps_o[0:BJ * T, 0:p], onehot[0:p, q, :, :].rearrange("p j t -> p (j t)"), p)\
                    .then_inc(s_ohT_ps, 1)
                pe.wait_ge(s_xT, 2 * b + 2)
                pe.wait_ge(s_al_used, b)
                for j in range(BJ):
                    last = nc.tensor.matmul(ps_a[0:p, j * T:(j + 1) * T], lhsT=xT[:, q, j * P:j * P + p],
                                            rhs=V_dst[:, :], start=True, stop=True)
                last.then_inc(s_al, 1)
                pe.wait_ge(s_ohT, b + 1)
                for h in range(2):
                    pe.wait_ge(s_bsel_used, 2 * b)
                    nc.tensor.matmul(ps_b[h][0:p, :], lhsT=onehotT[:, q, 0:p],
                                     rhs=bias_diag[:, h * 4 * C:(h + 1) * 4 * C], start=True, stop=True)\
                        .then_inc(s_bsel, 1)

            for b in range(SLOTS):
                node_block(b, 0, b, P)
            with pe.Fori(1, BLOCK_LOOPS) as i:
                for k in range(SLOTS):
                    node_block(SLOTS * i + k, i, k, P)
            for b in range(SLOTS * BLOCK_LOOPS, BLOCKS):
                node_block(b, b // SLOTS, b % SLOTS, P if b < FULL_BLOCKS else TAIL_P)

            pe.wait_ge(s_ohT, BLOCKS)
            pe.wait_ge(s_al_used, BLOCKS)
            pe.wait_ge(s_bsel_used, 2 * BLOCKS)

            def source_scores(g, i, k):
                q = k % 2
                pe.wait_ge(s_staged, g + 1)
                pe.wait_ge(e_accT, back(2 * g, 2))
                for h, (lo, hi) in enumerate(((0, 4), (4, U))):
                    for u in range(lo, hi):
                        last = transpose(ps_x[h][:, (u - lo) * P:(u - lo + 1) * P], xst[:, q, u, :], P)
                    last.then_inc(e_xT_ps, 1)
                pe.wait_ge(e_oh, g + 1)
                pe.wait_ge(e_ohT, g)
                transpose(ps_o[0:U * T, 0:P], onehot[:, q, 0:U, :].rearrange("p j t -> p (j t)"), P)\
                    .then_inc(e_ohT_ps, 1)
                pe.wait_ge(e_xT, 2 * g + 2)
                pe.wait_ge(e_al_used, g)
                for u in range(U):
                    last = nc.tensor.matmul(ps_a[:, u * T:(u + 1) * T], lhsT=xT[:, q, u * P:(u + 1) * P],
                                            rhs=V_src[:, :], start=True, stop=True)
                last.then_inc(e_al, 1)

            def apply_w(g, k):
                q = k % 2
                pe.wait_ge(e_xT, 2 * g + 4 if not isinstance(g, int) else min(2 * g + 4, 2 * GROUPS))
                for h, (lo, hi) in enumerate(((0, 4), (4, U))):
                    pe.wait_ge(e_acc, U * g + hi)
                    for u in range(lo, hi):
                        last = transpose(ps_x[h][:, (u - lo) * P:(u - lo + 1) * P], acc[:, q, u, :], P)
                    last.then_inc(e_accT_ps, 1)
                pe.wait_ge(e_ohT, g + 1)
                for h, (lo, hi) in enumerate(((0, 4), (4, U))):
                    pe.wait_ge(e_bsel_used, 2 * g)
                    nc.tensor.matmul(ps_b[h][:, 0:(hi - lo) * C], lhsT=onehotT[0:U * T, q, :],
                                     rhs=bias_diag[0:U * T, lo * C:hi * C], start=True, stop=True)\
                        .then_inc(e_bsel, 1)
                pe.wait_ge(e_accT, 2 * g + 2)
                for u in range(U):
                    pe.wait_ge(e_w_used, back(U * g + u, 1))
                    nc.tensor.matmul(ps_w[u % 2][:, 0:T * C], lhsT=accT[:, u * P:(u + 1) * P],
                                     rhs=W3[:, :, :].rearrange("p t c -> p (t c)"), start=True, stop=True)\
                        .then_inc(e_w, 1)

            source_scores(0, 0, 0)
            source_scores(1, 0, 1)
            for g in range(1, 4):
                apply_w(g - 1, g - 1)
                source_scores(g + 1, (g + 1) // SLOTS, (g + 1) % SLOTS)
            with pe.Fori(1, GROUPS // SLOTS - 1) as i:
                for k in range(SLOTS):
                    g = SLOTS * i + k
                    apply_w(g - 1, (k + 3) % SLOTS)
                    source_scores(g + 1, i + (1 if k == 3 else 0), (k + 1) % SLOTS)
            for g in range(GROUPS - SLOTS, GROUPS + 1):
                apply_w(g - 1, (g - 1) % SLOTS)
                if g + 1 < GROUPS:
                    source_scores(g + 1, (g + 1) // SLOTS, (g + 1) % SLOTS)

            pe.wait_ge(f_dve, 1)
            for c in range(5):
                last = transpose(ps_x[c // 4][0:1, (c % 4) * P:(c % 4 + 1) * P], cols[:, c:c + 1], P)
            last.then_inc(f_pe, 1)
            transpose(ps_w[0][:, 0:P], acc[:, (GROUPS - 1) % 2, U - 1, :], P)
            transpose(ps_w[0][:, P:2 * P], head_acc[:, :], P).then_inc(f_pe, 1)
            pe.wait_ge(f_dve, 3)
            nc.tensor.matmul(ps_b[0][:, :], lhsT=ones[0:1, :], rhs=xT[0:1, 1, 0:4 * P], start=True, stop=True)
            nc.tensor.matmul(ps_b[1][:, 0:1], lhsT=xT[0:1, 1, 4 * P:5 * P], rhs=ones[0:1, 0:1],
                             start=True, stop=True).then_inc(f_pe, 1)
            pe.wait_ge(f_rows, 16)
            transpose(ps_o[0:T, 0:P], rows[:, 0, 0, C + 1:ROW], P).then_inc(f_pe, 1)
            pe.wait_ge(f_dve, 4)
            nc.tensor.matmul(ps_w[1][:, 0:T * C], lhsT=accT[:, 0:P], rhs=W3[:, :, :].rearrange("p t c -> p (t c)"),
                             start=True, stop=True).then_inc(f_pe, 1)
            pe.wait_ge(f_act, 2)
            nc.tensor.matmul(ps_a[:, 0:C], lhsT=onehotT[0:T, 0, :], rhs=bias_diag[0:T, 0:C],
                             start=True, stop=True).then_inc(f_pe, 1)

        @block.scalar
        def _(act):
            def copy(o, i):
                return nc.scalar.activation(o, i, ACT.Copy)

            def normalise(o, zz, q, n, p, done):
                for j in range(n):
                    last = nc.scalar.activation(o[0:p, j, :], zz[0:p, j, :], ACT.Identity,
                                                bias=nbias[0:p, q, j:j + 1], scale=rstd[0:p, q, j:j + 1])
                last.then_inc(done, 1)

            act.wait_ge(s_setC, 2)

            def transposes_out(b, i, k, p):
                q = k % 2
                act.wait_ge(s_onehot, b + 1)
                act.wait_ge(s_row_out[k], 16 * i)
                copy(rows[0:p, k, :, C + 1:ROW], onehot[0:p, q, :, :]).then_inc(s_row_oh, 1)
                for h in range(2):
                    act.wait_ge(s_xT_ps, 2 * b + h + 1)
                    if h == 0:
                        act.wait_ge(s_al, back(b, 1))
                    copy(xT[:, q, h * 512:(h + 1) * 512].rearrange("c (j p) -> c j p", p=P)[:, :, 0:p],
                         ps_x[h][:, :].rearrange("c (j p) -> c j p", p=P)[:, :, 0:p]).then_inc(s_xT, 1)
                act.wait_ge(s_ohT_ps, b + 1)
                act.wait_ge(s_bsel, back(2 * b, 2))
                copy(onehotT[:, q, 0:p], ps_o[0:BJ * T, 0:p]).then_inc(s_ohT, 1)

            def layer_norm(b, i, k, p):
                q = k % 2
                act.wait_ge(s_var, b + 1)
                nc.scalar.activation(std[0:p, q, :], st[0:p, q, 4, :], ACT.Sqrt, bias=eps[0:p, :]).then_inc(s_std, 1)
                act.wait_ge(s_norm_par, b + 1)
                act.wait_ge(s_out[k], 16 * i)
                normalise(obuf[:, k], z[:, q], q, BJ, p, s_norm)

            transposes_out(0, 0, 0, P)
            for b in range(1, SLOTS):
                transposes_out(b, 0, b, P)
                layer_norm(b - 1, 0, b - 1, P)
            with act.Fori(1, BLOCK_LOOPS) as i:
                for k in range(SLOTS):
                    transposes_out(SLOTS * i + k, i, k, P)
                    layer_norm(SLOTS * i + k - 1, i - (1 if k == 0 else 0), (k + 3) % SLOTS, P)
            for b in range(SLOTS * BLOCK_LOOPS, BLOCKS + 1):
                if b < BLOCKS:
                    transposes_out(b, b // SLOTS, b % SLOTS, P if b < FULL_BLOCKS else TAIL_P)
                layer_norm(b - 1, (b - 1) // SLOTS, (b - 1) % SLOTS, P if b - 1 < FULL_BLOCKS else TAIL_P)

            act.wait_ge(s_idx, 1)
            act.wait_ge(s_al, BLOCKS)
            act.wait_ge(s_bsel, 2 * BLOCKS)
            for k in range(SLOTS):
                act.wait_ge(s_out[k], 16 * ((BLOCKS - 1 - k) // SLOTS + 1))

            def stage(g, slot, k):
                act.wait_ge(s_xs, g + 1)
                act.wait_ge(e_xT_ps, back(2 * g, 2))
                act.wait_ge(e_px, back(U * g, U))
                copy(xst[:, k % 2, :, :].rearrange("p u c -> p (u c)"), xs_ring[:, slot, :]).then_inc(s_staged, 1)

            def source_out(g, i, k):
                q = k % 2
                act.wait_ge(s_gr[k], 16 * U * (i + 1))
                copy(onehot[:, q, 0:U, :], rows[:, k, 0:U, C + 1:ROW]).then_inc(e_oh, 1)
                act.wait_ge(e_al, back(g, 1))
                for h, (lo, hi) in enumerate(((0, 4), (4, U))):
                    act.wait_ge(e_xT_ps, 2 * g + h + 1)
                    copy(xT[:, q, lo * P:hi * P], ps_x[h][:, 0:(hi - lo) * P]).then_inc(e_xT, 1)
                act.wait_ge(e_ohT_ps, g + 1)
                act.wait_ge(e_bsel, back(2 * g, 2))
                copy(onehotT[0:U * T, q, :], ps_o[0:U * T, 0:P]).then_inc(e_ohT, 1)

            def acc_out(g):
                act.wait_ge(e_w, U * g)
                for h, (lo, hi) in enumerate(((0, 4), (4, U))):
                    act.wait_ge(e_accT_ps, 2 * g + h + 1)
                    copy(accT[:, lo * P:hi * P], ps_x[h][:, 0:(hi - lo) * P]).then_inc(e_accT, 1)

            def weights(g, k):
                q = k % 2
                act.wait_ge(e_expo, g + 1)
                nc.scalar.activation(fp[:, q, :, :], expo[:, q, :, :], ACT.Exp).then_inc(e_exp, 1)
                act.wait_ge(e_exp, g + 1)
                act.wait_ge(e_acc, U * g)
                for u in range(U):
                    nc.scalar.activation(px[:, u, :], xst[:, q, u, :], ACT.Copy,
                                         scale=fp[:, q, 1, u:u + 1]).then_inc(e_px, 1)

            def edge_norm(g, i, k):
                q = k % 2
                act.wait_ge(e_var, g + 1)
                nc.scalar.activation(std[:, q, 0:U], st[:, q, 4, 0:U], ACT.Sqrt, bias=eps[:, :]).then_inc(e_std, 1)
                act.wait_ge(e_norm_par, g + 1)
                act.wait_ge(s_sc[k], 16 * U * i)
                normalise(obuf[:, k], z[:, q], q, U, P, e_norm)

            def one(g, i, k, before, after):
                if after:
                    stage(g + 1, (g + 1) % RING, (k + 1) % SLOTS)
                if before:
                    acc_out(g - 1)
                if g is not None and (not isinstance(g, int) or g < GROUPS):
                    weights(g, k)
                if after:
                    source_out(g + 1, i + (1 if k == SLOTS - 1 else 0), (k + 1) % SLOTS)
                if before:
                    edge_norm(g - 1, i - (1 if k == 0 else 0), (k + 3) % SLOTS)

            stage(0, 0, 0)
            source_out(0, 0, 0)
            for g in range(SLOTS):
                one(g, 0, g, g > 0, True)
            with act.Fori(1, GROUPS // SLOTS - 1) as i:
                for k in range(SLOTS):
                    one(SLOTS * i + k, i, k, True, True)
            for g in range(GROUPS - SLOTS, GROUPS + 1):
                one(g, g // SLOTS, g % SLOTS, True, g + 1 < GROUPS)

            act.wait_ge(f_dve, 2)
            nc.scalar.activation(xT[0:1, 1, 0:4 * P], xT[0:1, 0, 0:4 * P], ACT.Exp).then_inc(f_act, 1)
            act.wait_ge(f_pe, 4)
            copy(onehotT[0:T, 0, :], ps_o[0:T, 0:P]).then_inc(f_act, 1)
            act.wait_ge(f_dve, 5)
            nc.scalar.activation(std[:, 0, 0:1], st[:, 0, 4, 0:1], ACT.Sqrt, bias=eps[:, :]).then_inc(f_act, 1)
            act.wait_ge(f_dve, 6)
            act.wait_ge(s_sc[0], 16 * U * (GROUPS // SLOTS))
            normalise(obuf[:, 0], z[:, 0], 0, 1, P, f_act)

        @block.vector
        def _(dve):
            tt = nc.vector.tensor_tensor
            ts = nc.vector.tensor_scalar
            stt = nc.vector.scalar_tensor_tensor

            class Order:

                def __init__(self, sem, base, total=None):
                    self.sem, self.base, self.total, self.n = sem, base, total, 0

                def done(self, instruction):
                    instruction.then_inc(self.sem, 1)
                    self.n += 1
                    return self.base + self.n

                def wait(self):
                    dve.wait_ge(self.sem, self.base + self.n)

                def link(self, instruction):
                    self.done(instruction)
                    self.wait()

                def end(self):
                    assert self.total in (None, self.n), self.n

            o = Order(s_dve_setup, 0)
            for v, value in ((eps[:, :], EPS), (M_all[:, 0:1], -BIG), (S_all[:, 0:1], 0.0),
                             (acc[:, 1, U - 1, :], 0.0), (head_acc[:, :], 0.0)):
                o.done(nc.vector.memset(v, value))
            dve.wait_ge(s_const, 3)
            dve.wait_ge(s_par, 16 * PAR_LOADS)
            for t in range(T):
                o.done(ts(a_edge_bc[:, t, :], ones[:, :], a_edge[:, t:t + 1], None, ALU.mult))
            dve.wait_ge(s_setT, 1)
            o.done(nc.vector.tensor_copy(WT[:, :, :].rearrange("p t c -> p (t c)"), ps_x[0][:, 0:T * C]))
            o.wait()
            nc.vector.tensor_copy(WeT[:, :, :].rearrange("p t c -> p (t c)"), ps_x[1][:, 0:T * ED])\
                .then_inc(s_setC, 1)
            dve.wait_ge(s_setT, 2)
            o.done(nc.vector.tensor_copy(V_src[:, :], ps_a[:, 0:T]))
            o.done(nc.vector.tensor_copy(V_dst[:, :], ps_a[:, T:2 * T]))
            o.wait()
            nc.vector.tensor_copy(g_edge[:, :, :].rearrange("p t c -> p (t c)"), ps_a[:, 64:64 + T * ED])\
                .then_inc(s_setC, 1)
            dve.wait_ge(s_setC, 2)

            def edge_scores(c):
                h = c % 2
                loads = [3 if min((k + 1) * ATTR_CHUNK, LAST_LANE) > k * ATTR_CHUNK else 2 for k in range(4)]
                dve.wait_ge(s_attr[h], 16 * sum(loads[h:c + 1:2]))
                for t in range(T):
                    o.link(tt(attr_prod, attr_c[h],
                              g_edge[:, t, :].unsqueeze(1).to_broadcast([P, ATTR_CHUNK, ED]), ALU.mult))
                    o.link(nc.vector.tensor_reduce(edge_score[:, c * ATTR_CHUNK:(c + 1) * ATTR_CHUNK, t],
                                                   attr_prod, X_AXIS, ALU.add))
                dve.sem_inc(s_attr_used, 1)

            for c in range(4):
                edge_scores(c)

            dve.wait_ge(s_dst, 16 * 9)
            for f, i in ((dF, dI), (nF, nI), (pF, pI)):
                o.done(nc.vector.tensor_copy(f, i))
            o.wait()
            last = LANE_EDGES - 1
            carries, inner, ends_here, fix = (cin[:, c:c + 1] for c in range(4))
            o.done(ts(hd, dF, dF[:, 0:1], None, ALU.is_equal))
            o.done(tt(carries, pF[:, 0:1], dF[:, 0:1], ALU.is_equal))
            o.done(tt(restart[:, :], pF, dF, ALU.not_equal))
            o.wait()
            o.done(ts(restart[:, :], restart[:, :], -BIG, None, ALU.mult))
            o.done(tt(pF, nF, dF, ALU.not_equal))
            o.wait()
            o.done(nc.vector.memset(restart[:, 0:1], -BIG))
            o.done(tt(head_end[:, 0:last], hd[:, 0:last], pF[:, 0:last], ALU.mult))
            o.done(nc.vector.tensor_copy(head_end[:, last:], hd[:, last:]))
            o.done(tt(cols[:, 4:5], carries, hd[:, last:], ALU.mult))
            o.done(ts(nF, hd, carries, None, ALU.mult))
            o.done(ts(inner, pF[:, last:], -1.0, 1.0, ALU.mult, ALU.add))
            o.wait()
            o.done(ts(nF, nF, -1.0, 1.0, ALU.mult, ALU.add))
            o.done(tt(inner, inner, hd[:, last:], ALU.mult))
            o.wait()
            o.done(tt(nF, nF, pF, ALU.mult))
            o.done(ts(ends_here, inner, -1.0, 1.0, ALU.mult, ALU.add))
            o.wait()
            o.done(ts(nF, nF, -float(SKIP), float(SKIP), ALU.mult, ALU.add))
            o.done(tt(fix, ends_here, carries, ALU.mult))
            o.wait()
            o.done(tt(out_idx[:, :], nF, dF, ALU.add))
            o.done(ts(fix, fix, -float(SKIP), float(SKIP), ALU.mult, ALU.add))
            o.done(ts(row_idx[:, :], dF, float(N - 1), None, ALU.min))
            o.wait()
            o.link(tt(fix_idx[:, :], fix, dF[:, 0:1], ALU.add))
            dve.sem_inc(s_idx, 1)

            def statistics(o, q, n, p, done):
                for j in range(n):
                    o.done(nc.vector.bn_stats(stats[0:p, q, j, :], z[0:p, q, j, :]))
                o.wait()
                f = lambda c: stats[0:p, q, 0:n, c]
                v = lambda c: st[0:p, q, c, 0:n]
                o.done(tt(v(0), f(1), f(4), ALU.add))
                o.done(tt(v(1), f(1), f(4), ALU.subtract))
                o.done(tt(v(2), f(2), f(5), ALU.add))
                o.wait()
                o.link(stt(v(3), v(1), 0.25, v(1), ALU.mult, ALU.mult))
                stt(v(4), v(2), 1.0 / C, v(3), ALU.mult, ALU.add).then_inc(done, 1)

            def norm_parameters(o, q, n, p, done):
                o.link(nc.vector.reciprocal(rstd[0:p, q, 0:n], std[0:p, q, 0:n]))
                stt(nbias[0:p, q, 0:n], st[0:p, q, 0, 0:n], -0.5, rstd[0:p, q, 0:n], ALU.mult, ALU.mult)\
                    .then_inc(done, 1)

            dve.wait_ge(s_types, 32)

            def node_onehot(b, i, k, p):
                o = Order(s_node_oh, 3 * b, 3)
                dve.wait_ge(s_ohT_ps, back(b, 1))
                dve.wait_ge(s_row_oh, back(b, 1))
                ty = types[0:p, b, :]
                one = lambda t: onehot[0:p, k % 2, :, t]
                o.done(ts(one(0), ty, 0.0, None, ALU.is_equal))
                o.done(ts(one(1), ty, 1.0, None, ALU.is_equal))
                o.wait()
                o.link(tt(types1h[0:p, :], one(0), one(1), ALU.add))
                o.end()
                ts(one(2), types1h[0:p, :], -1.0, 1.0, ALU.mult, ALU.add).then_inc(s_onehot, 1)

            def node_score(b, i, k, p):
                dve.wait_ge(s_al, b + 1)
                dve.wait_ge(s_onehot, b + 1)
                tt(prod[0:p, :, :], ps_a[0:p, 0:BJ * T].rearrange("p (j t) -> p j t", t=T),
                   onehot[0:p, k % 2, :, :], ALU.mult).then_inc(s_al_used, 1)
                dve.wait_ge(s_al_used, b + 1)
                dve.wait_ge(s_row_out[k], 16 * i)
                nc.vector.tensor_reduce(rows[0:p, k, :, C], prod[0:p, :, :], X_AXIS, ALU.add)\
                    .then_inc(s_rows_full, 1)

            def node_z(b, i, k, p):
                q = k % 2
                dve.wait_ge(s_norm, back(b, 1))
                dve.wait_ge(s_row_in[k], 16 * (i + 1))
                for h in range(2):
                    dve.wait_ge(s_bsel, 2 * b + h + 1)
                    tt(z[0:p, q, 4 * h:4 * h + 4, :], ps_b[h][0:p, :].rearrange("p (j c) -> p j c", c=C),
                       rows[0:p, k, 4 * h:4 * h + 4, 0:C], ALU.add).then_inc(s_bsel_used, 1)
                dve.wait_ge(s_bsel_used, 2 * b + 2)
                stt(z[0:p, q, :, :], z[0:p, q, :, :], 0.0, rows[0:p, k, :, 0:C], ALU.max, ALU.add).then_inc(s_z, 1)
                dve.wait_ge(s_z, b + 1)
                o = Order(s_node_st, 12 * b, 12)
                statistics(o, q, BJ, p, s_var)
                o.end()

            def node_norm(b, k, p):
                dve.wait_ge(s_std, b + 1)
                norm_parameters(Order(s_node_np, b, 1), k % 2, BJ, p, s_norm_par)

            def node_step(b, i, k, p, before):
                node_onehot(b, i, k, p)
                node_score(b, i, k, p)
                if before:
                    node_norm(b - 1, (k + 3) % SLOTS, before)
                node_z(b, i, k, p)

            for b in range(SLOTS):
                node_step(b, 0, b, P, P if b else 0)
            with dve.Fori(1, BLOCK_LOOPS) as i:
                for k in range(SLOTS):
                    node_step(SLOTS * i + k, i, k, P, P)
            for b in range(SLOTS * BLOCK_LOOPS, BLOCKS):
                node_step(b, b // SLOTS, b % SLOTS, P if b < FULL_BLOCKS else TAIL_P, P)
            node_norm(BLOCKS - 1, (BLOCKS - 1) % SLOTS, TAIL_P)

            dve.wait_ge(s_norm, BLOCKS)

            def columns(t, g, n=U):
                return t[:, bass.ds(g * U, n)]

            def scores(g, i, k):
                q = k % 2
                o = Order(e_dve_a, 7 * g, 7)
                sc = score[:, q, 0:U]
                dve.wait_ge(s_gr[k], 16 * U * (i + 1))
                dve.wait_ge(e_al, g + 1)
                tt(prod[:, 0:U, :], ps_a[:, 0:U * T].rearrange("p (j t) -> p j t", t=T),
                   edge_score[:, bass.ds(g * U, U), :], ALU.add).then_inc(e_al_used, 1)
                dve.wait_ge(e_al_used, g + 1)
                o.link(tt(prod[:, 0:U, :], prod[:, 0:U, :], rows[:, k, 0:U, C + 1:ROW], ALU.mult))
                o.link(nc.vector.tensor_reduce(sc, prod[:, 0:U, :], X_AXIS, ALU.add))
                o.link(tt(sc, sc, rows[:, k, 0:U, C], ALU.add))
                o.link(stt(sc, sc, 0.2, sc, ALU.mult, ALU.max))
                M_new = M_all[:, bass.ds(g * U + 1, U)]
                o.link(nc.vector.tensor_tensor_scan(M_new, columns(restart, g), sc, columns(M_all, g, 1),
                                                    ALU.add, ALU.max))
                o.link(tt(expo[:, q, 0, :], columns(M_all, g), columns(restart, g), ALU.add))
                o.link(tt(expo[:, q, 0, :], expo[:, q, 0, :], M_new, ALU.subtract))
                o.end()
                tt(expo[:, q, 1, :], sc, M_new, ALU.subtract).then_inc(e_expo, 1)

            def accumulate(g, i, k):
                q = k % 2
                o = Order(e_dve_b, 4 * g, 4)
                dve.wait_ge(e_exp, g + 1)
                S_new = S_all[:, bass.ds(g * U + 1, U)]
                o.link(nc.vector.tensor_tensor_scan(S_new, fp[:, q, 0, :], fp[:, q, 1, :], columns(S_all, g, 1),
                                                    ALU.mult, ALU.add))
                dve.wait_ge(e_accT_ps, back(2 * g, 2))
                dve.wait_ge(e_head, U * g)

                def keep_head(u):
                    dve.wait_ge(e_acc, U * g + u + 1)
                    dve.wait_ge(e_head, U * g + u)
                    stt(head_acc[:, :], acc[:, q, u, :], head_end[:, bass.ds(g * U + u, 1)], head_acc[:, :],
                        ALU.mult, ALU.add).then_inc(e_head, 1)

                for u in range(U):
                    before = acc[:, q, u - 1, :] if u else acc[:, 1 - q, U - 1, :]
                    dve.wait_ge(e_px, U * g + u + 1)
                    dve.wait_ge(e_acc, U * g + u)
                    stt(acc[:, q, u, :], before, fp[:, q, 0, u:u + 1], px[:, u, :], ALU.mult, ALU.add)\
                        .then_inc(e_acc, 1)
                    if u:
                        keep_head(u - 1)
                keep_head(U - 1)
                o.link(ts(rs[:, 0:U], S_new, TINY, None, ALU.add))
                o.link(nc.vector.reciprocal(rs[:, 0:U], rs[:, 0:U]))
                o.link(tt(kk[:, q, :, :], rows[:, k, 0:U, C + 1:ROW],
                          rs[:, 0:U].unsqueeze(2).to_broadcast([P, U, T]), ALU.mult))
                o.end()

            def outputs(g, k):
                q = k % 2
                dve.wait_ge(e_norm, back(g, 1))
                for h, (lo, hi) in enumerate(((0, 4), (4, U))):
                    dve.wait_ge(e_bsel, 2 * g + h + 1)
                    tt(z[:, q, lo:hi, :], ps_b[h][:, 0:(hi - lo) * C].rearrange("p (j c) -> p j c", c=C),
                       rows[:, k, lo:hi, 0:C], ALU.add).then_inc(e_bsel_used, 1)
                dve.wait_ge(e_bsel_used, 2 * g + 2)
                o = Order(e_dve_c, 14 * g + 11 * g, 25)
                before = {}
                for us in ((0, 1), (2, 3), (4, 5), (6,)):
                    for t in range(T):
                        for u in us:
                            if t == 0:
                                dve.wait_ge(e_w, U * g + u + 1)
                            else:
                                dve.wait_ge(e_dve_c, before[u])
                            ins = stt(z[:, q, u, :], ps_w[u % 2][:, t * C:(t + 1) * C], kk[:, q, u, t:t + 1],
                                      z[:, q, u, :], ALU.mult, ALU.add)
                            if t < T - 1:
                                before[u] = o.done(ins)
                            else:
                                ins.then_inc(e_w_used, 1)
                dve.wait_ge(e_w_used, U * g + U)
                stt(z[:, q, 0:U, :], z[:, q, 0:U, :], 0.0, rows[:, k, 0:U, 0:C], ALU.max, ALU.add).then_inc(e_z, 1)
                dve.wait_ge(e_z, g + 1)
                statistics(o, q, U, P, e_var)
                o.end()

            def norms(g, k):
                dve.wait_ge(e_std, g + 1)
                norm_parameters(Order(e_dve_n, g, 1), k % 2, U, P, e_norm_par)

            def edge_step(g, i, k):
                before = (k + 3) % SLOTS
                scores(g, i, k)
                outputs(g - 1, before)
                accumulate(g, i, k)
                norms(g - 1, before)

            scores(0, 0, 0)
            accumulate(0, 0, 0)
            for g in range(1, SLOTS):
                edge_step(g, 0, g)
            with dve.Fori(1, GROUPS // SLOTS) as i:
                for k in range(SLOTS):
                    edge_step(SLOTS * i + k, i, k)
            outputs(GROUPS - 1, SLOTS - 1)
            norms(GROUPS - 1, SLOTS - 1)

            o = Order(s_dve_last, 0)
            dve.wait_ge(e_norm, GROUPS)
            dve.wait_ge(e_z, GROUPS)
            hM = px[:, 0:4, :].rearrange("p a c -> p (a c)")[:, 0:LANE_EDGES]
            for c, v in ((2, M_all), (3, S_all)):
                o.link(tt(hM, v[:, 1:], head_end[:, :], ALU.mult))
                o.link(nc.vector.tensor_reduce(cols[:, c:c + 1], hM, X_AXIS, ALU.add))
                o.link(nc.vector.tensor_copy(cols[:, c - 2:c - 1], v[:, LANE_EDGES:]))
            dve.sem_inc(f_dve, 1)

            row = z[0:1, 1, :, :].rearrange("p a c -> p (a c)")
            tailM, tailS, headM, headS, through = (row[:, c * P:(c + 1) * P] for c in range(5))
            Kbuf, Sbuf = xT[0:1, 0, 512:512 + P + 1], xT[0:1, 0, 704:704 + P + 1]
            headMx, headSx = row[:, 5 * P:6 * P], row[:, 6 * P:7 * P]
            factor = lambda j: xT[0:1, 0, j * P:(j + 1) * P]
            expd = lambda j: xT[0:1, 1, j * P:(j + 1) * P]
            dve.wait_ge(f_pe, 2)
            o.done(nc.vector.tensor_copy(row[:, 0:4 * P], ps_x[0][0:1, :]))
            o.done(ts(through, ps_x[1][0:1, 0:P], -1.0, BIG, ALU.add, ALU.mult))
            o.done(nc.vector.memset(Kbuf[:, 0:1], -BIG))
            o.done(nc.vector.memset(Sbuf[:, 0:1], 0.0))
            o.wait()
            o.link(nc.vector.tensor_tensor_scan(Kbuf[:, 1:], through, tailM, -BIG, ALU.add, ALU.max))
            o.link(tt(factor(0), Kbuf[:, 0:P], through, ALU.add))
            o.link(tt(factor(0), factor(0), Kbuf[:, 1:], ALU.subtract))
            o.link(tt(factor(1), tailM, Kbuf[:, 1:], ALU.subtract))
            o.link(tt(headMx, Kbuf[:, 0:P], headM, ALU.max))
            o.link(tt(factor(2), Kbuf[:, 0:P], headMx, ALU.subtract))
            o.link(tt(factor(3), headM, headMx, ALU.subtract))
            dve.sem_inc(f_dve, 1)
            dve.wait_ge(f_act, 1)
            o.link(tt(tailS, tailS, expd(1), ALU.mult))
            o.link(nc.vector.tensor_tensor_scan(Sbuf[:, 1:], expd(0), tailS, 0.0, ALU.mult, ALU.add))
            o.link(tt(headSx, Sbuf[:, 0:P], expd(2), ALU.mult))
            o.link(tt(headS, headS, expd(3), ALU.mult))
            o.link(tt(headS, headS, headSx, ALU.add))
            o.link(ts(headS, headS, TINY, None, ALU.add))
            o.link(nc.vector.reciprocal(expd(4), headS))
            dve.sem_inc(f_dve, 1)

            dve.wait_ge(f_pe, 3)
            bc = lambda j: xT[:, 0, j * P:(j + 1) * P]
            carry = px[:, 0:2, :].rearrange("p a c -> p (a c)")[:, 0:P + 1]
            whole = accT[:, 0:P]
            o.done(nc.vector.tensor_copy(xT[:, 0, 0:4 * P], ps_b[0][:, :]))
            o.done(nc.vector.tensor_copy(rs[:, 0:1], ps_b[1][:, 0:1]))
            o.done(nc.vector.memset(carry[:, 0:1], 0.0))
            o.wait()
            o.link(tt(bc(1), ps_w[0][:, 0:P], bc(1), ALU.mult))
            o.link(nc.vector.tensor_tensor_scan(carry[:, 1:], bc(0), bc(1), 0.0, ALU.mult, ALU.add))
            o.link(tt(bc(3), ps_w[0][:, P:2 * P], bc(3), ALU.mult))
            o.link(tt(bc(2), carry[:, 0:P], bc(2), ALU.mult))
            o.link(tt(whole, bc(2), bc(3), ALU.add))
            dve.sem_inc(f_dve, 1)

            dve.wait_ge(f_rows, 16)
            o.link(ts(kk[:, 0, 0, :], rows[:, 0, 0, C + 1:ROW], rs[:, 0:1], None, ALU.mult))
            dve.wait_ge(f_pe, 6)
            o.link(tt(z[:, 0, 0, :], ps_a[:, 0:C], rows[:, 0, 0, 0:C], ALU.add))
            for t in range(T):
                o.link(stt(z[:, 0, 0, :], ps_w[1][:, t * C:(t + 1) * C], kk[:, 0, 0, t:t + 1], z[:, 0, 0, :],
                           ALU.mult, ALU.add))
            o.link(stt(z[:, 0, 0, :], z[:, 0, 0, :], 0.0, rows[:, 0, 0, 0:C], ALU.max, ALU.add))
            statistics(o, 0, 1, P, f_dve)
            dve.wait_ge(f_act, 3)
            norm_parameters(o, 0, 1, P, f_dve)


_PARAMS = ("W", "as", "ad", "We", "ae", "b")


def kernel(**inputs):
    import numpy as np
    import concourse.bacc as bacc
    from concourse.bass_utils import run_bass_kernel_spmd

    nc = bacc.Bacc("TRN2", target_bir_lowering=False, num_devices=1)
    arrays = {}

    def given(name):
        a = np.ascontiguousarray(inputs[name])
        arrays[f"in_{name}_dram"] = a
        return nc.dram_tensor(f"in_{name}_dram", a.shape, mybir.dt.from_np(a.dtype), kind="ExternalInput").ap()

    graph = [given(name) for name in ("x", "src", "dst", "edge_attr_16", "node_type_3")]
    convs = [[given(f"L0_gnn_{p}{c}") for p in _PARAMS] for c in "vri"]
    shape = inputs["x"].shape
    out = nc.dram_tensor("out_0_dram", shape, mybir.dt.float32, kind="ExternalOutput").ap()
    gat_kernel(nc, *graph, convs, out)
    r = run_bass_kernel_spmd(nc, [arrays], core_ids=[0])
    return r.results[0]["out_0_dram"]
```

```python
import concourse.bass as bass
from concourse import mybir
from contextlib import ExitStack


def gat_kernel(nc, x, src, dst, edge_attr, node_type, convs, out):
    fp32 = mybir.dt.float32
    i32 = mybir.dt.int32
    bf16 = mybir.dt.bfloat16
    ALU = mybir.AluOpType
    ACT = mybir.ActivationFunctionType
    X_AXIS = mybir.AxisListType.X

    N, C = x.shape
    E, ED = edge_attr.shape
    P = 128
    T = 3
    BIG = 1.0e30
    EPS = 1e-5
    TINY = 1e-16

    BJ = 8
    BLOCK = P * BJ
    FULL_BLOCKS = N // BLOCK
    TAIL_P = (N - FULL_BLOCKS * BLOCK) // BJ
    BLOCKS = FULL_BLOCKS + 1
    assert FULL_BLOCKS * BLOCK + TAIL_P * BJ == N
    SLOTS = 4
    BLOCK_LOOPS = FULL_BLOCKS // SLOTS

    U = 7
    LANE_EDGES = -(-E // (P * U * SLOTS)) * U * SLOTS
    GROUPS = LANE_EDGES // U
    FULL_LANES = E // LANE_EDGES
    LAST_LANE = E - FULL_LANES * LANE_EDGES
    assert FULL_LANES == P - 1 and 1 < LAST_LANE < LANE_EDGES
    PAD_DST = 1 << 17
    SKIP = 1 << 18
    assert N < PAD_DST
    RING = GROUPS // 2
    ROW = C + 1 + T
    LAG = 4
    ATTR_CHUNK = LANE_EDGES // 4

    def back(count, n):
        return max(count - n, 0) if isinstance(count, int) else count - n

    node_rows = nc.dram_tensor("node_rows", (N, ROW), fp32).ap()
    acc_rows = nc.dram_tensor("acc_rows", (P * LANE_EDGES, C), fp32).ap()
    REP = 32

    def first_rows(t, n, p):
        return t[bass.ds(n, p * BJ), :].rearrange("(p j) c -> p j c", j=BJ)

    with ExitStack() as ctx:
        def sb(name, shape, dt=fp32):
            return ctx.enter_context(nc.sbuf_tensor(name, shape, dt))

        def pb(name, n=512, dt=fp32):
            return ctx.enter_context(nc.psum_tensor(name, [P, n], dt))

        def sem(name):
            return ctx.enter_context(nc.semaphore(name))

        ident = sb("ident", [P, P])
        ident_b = sb("ident_b", [P, P], bf16)
        ones = sb("ones", [P, P])
        W3 = sb("W3", [P, T, C])
        WT = sb("WT", [P, T, C])
        We3 = sb("We3", [ED, T, C])
        WeT = sb("WeT", [P, T, ED])
        a_src = sb("a_src", [P, T])
        a_dst = sb("a_dst", [P, T])
        a_edge = sb("a_edge", [P, T])
        a_edge_bc = sb("a_edge_bc", [P, T, P])
        V_src = sb("V_src", [P, T])
        V_dst = sb("V_dst", [P, T])
        g_edge = sb("g_edge", [P, T, ED])
        bias_parts = sb("bias_parts", [T * REP, BJ * C], bf16)
        types = sb("types", [P, BLOCKS, BJ], i32)
        src_idx = sb("src_idx", [P, LANE_EDGES], i32)
        row_idx = sb("row_idx", [P, LANE_EDGES], i32)
        out_idx = sb("out_idx", [P, LANE_EDGES], i32)
        fix_idx = sb("fix_idx", [P, 1], i32)
        restart = sb("restart", [P, LANE_EDGES])
        head_end = sb("head_end", [P, LANE_EDGES])
        edge_score = sb("edge_score", [P, LANE_EDGES, T])
        M_all = sb("M_all", [P, LANE_EDGES + 1])
        S_all = sb("S_all", [P, LANE_EDGES + 1])
        xs_ring = sb("xs_ring", [P, RING, U * C])
        rows = sb("rows", [P, SLOTS, BJ, ROW])
        z = sb("z", [P, SLOTS, BJ, C])
        xT = sb("xT", [P, 2, BJ * C])
        onehot_all = sb("onehot_all", [P, BLOCKS, BJ, T], bf16)
        onehot3 = sb("onehot3", [P, 2, 3, REP], bf16)
        onehotT = sb("onehotT", [T * REP, 2, P], bf16)
        xst = sb("xst", [P, 2, U, C])
        px = sb("px", [P, U, C])
        acc = sb("acc", [P, 2, U, C])
        accT = sb("accT", [P, 2, U * C])
        head_acc = sb("head_acc", [P, C])
        prod = sb("prod", [P, 2, BJ, T])
        score = sb("score", [P, 2, BJ])
        expo = sb("expo", [P, 2, 2, U])
        fp = sb("fp", [P, 2, 2, U])
        rs = sb("rs", [P, BJ])
        kk = sb("kk", [P, 2, U, T])
        stats = sb("stats", [P, 2, 2 * BJ, 6])
        st = sb("st", [P, 2, 5, 2 * BJ])
        std = sb("std", [P, 2, 2 * BJ])
        rstd = sb("rstd", [P, 2, 2 * BJ])
        nbias = sb("nbias", [P, 2, 2 * BJ])
        lane_base = sb("lane_base", [P, 1], i32)
        head_idx = sb("head_idx", [P, 1], i32)
        eps = sb("eps", [P, 1])
        cols = sb("cols", [P, 6])
        cin = sb("cin", [P, 4])

        dI = acc[:, 0, 0:4, :].rearrange("p a c -> p (a c)")[:, 0:LANE_EDGES].bitcast(i32)
        nI = acc[:, 1, 0:4, :].rearrange("p a c -> p (a c)")[:, 0:LANE_EDGES].bitcast(i32)
        pI = xst[:, 0, 0:4, :].rearrange("p a c -> p (a c)")[:, 0:LANE_EDGES].bitcast(i32)
        dF = xst[:, 1, 0:4, :].rearrange("p a c -> p (a c)")[:, 0:LANE_EDGES]
        nF = accT[:, 0, 0:LANE_EDGES]
        pF = accT[:, 1, 0:LANE_EDGES]
        hd = px[:, 0:4, :].rearrange("p a c -> p (a c)")[:, 0:LANE_EDGES]
        bias_f = z[0:BJ * T, 0, :, :].rearrange("p a c -> p (a c)")
        bias_r = z[0:BJ * T, 1, :, :].rearrange("p a c -> p (a c)")
        bias_m = xT[0:BJ * T, 0, 0:BJ * C // 2].bitcast(bf16)
        attr_c = acc[:, :, :, :].rearrange("p q u c -> p (q u c)")[:, 0:ATTR_CHUNK * ED]\
            .rearrange("p (j d) -> p j d", d=ED)
        attr_prod = accT[:, :, :].rearrange("p q n -> p (q n)")[:, 0:ATTR_CHUNK * ED]\
            .rearrange("p (j d) -> p j d", d=ED)

        ps_x = [pb("ps_x0"), pb("ps_x1")]
        ps_b = [pb("ps_b0"), pb("ps_b1")]
        ps_w = [pb("ps_w0"), pb("ps_w1")]
        banks = [*ps_w, *ps_b]
        ps_a = pb("ps_a")
        ps_o = pb("ps_o", 1024, bf16)

        s_const = sem("s_const")
        s_par = sem("s_par")
        s_bias = sem("s_bias")
        s_pad = sem("s_pad")
        s_src = sem("s_src")
        s_dst = sem("s_dst")
        s_types = sem("s_types")
        s_attr = sem("s_attr")
        s_score = sem("s_score")
        s_onehots = sem("s_onehots")
        s_keep = [sem(f"s_keep{q}") for q in range(2)]
        s_rep = sem("s_rep")
        s_setT = sem("s_setT")
        s_setC = sem("s_setC")
        s_idx = sem("s_idx")
        s_row_in = [sem(f"s_row_in{k}") for k in range(SLOTS)]
        s_row_out = [sem(f"s_row_out{k}") for k in range(SLOTS)]
        s_out = [sem(f"s_out{k}") for k in range(SLOTS)]
        s_row_oh = sem("s_row_oh")
        s_rows_full = sem("s_rows_full")
        s_xT_ps = sem("s_xT_ps")
        s_xT = sem("s_xT")
        s_al = sem("s_al")
        s_al_used = sem("s_al_used")
        s_ohT_ps = sem("s_ohT_ps")
        s_ohT = sem("s_ohT")
        s_bsel = sem("s_bsel")
        s_bsel_used = sem("s_bsel_used")
        s_z = sem("s_z")
        s_var = sem("s_var")
        s_std = sem("s_std")
        s_norm_par = sem("s_norm_par")
        s_norm = sem("s_norm")
        s_gx = [sem(f"s_gx{k}") for k in range(SLOTS)]
        s_gr = [sem(f"s_gr{k}") for k in range(SLOTS)]
        s_sc = [sem(f"s_sc{k}") for k in range(SLOTS)]
        s_xs = sem("s_xs")
        s_staged = sem("s_staged")
        e_xT_ps = sem("e_xT_ps")
        e_xT = sem("e_xT")
        e_al = sem("e_al")
        e_al_used = sem("e_al_used")
        e_rep = sem("e_rep")
        e_ohT_ps = sem("e_ohT_ps")
        e_ohT = sem("e_ohT")
        e_expo = sem("e_expo")
        e_exp = sem("e_exp")
        e_px = sem("e_px")
        e_acc = sem("e_acc")
        e_accT_ps = sem("e_accT_ps")
        e_accT = sem("e_accT")
        e_w = sem("e_w")
        e_w_used = sem("e_w_used")
        e_bsel = sem("e_bsel")
        e_bsel_used = sem("e_bsel_used")
        e_z = sem("e_z")
        e_var = sem("e_var")
        e_std = sem("e_std")
        e_norm_par = sem("e_norm_par")
        e_norm = sem("e_norm")
        s_dve_setup = sem("s_dve_setup")
        s_node_al = sem("s_node_al")
        s_node_st = sem("s_node_st")
        s_node_np = sem("s_node_np")
        e_zero = sem("e_zero")
        e_dve_a = sem("e_dve_a")
        e_dve_b = sem("e_dve_b")
        e_dve_c = sem("e_dve_c")
        e_dve_n = sem("e_dve_n")
        s_dve_last = sem("s_dve_last")
        f_pe = sem("f_pe")
        f_dve = sem("f_dve")
        f_act = sem("f_act")
        f_rows = sem("f_rows")
        f_head = sem("f_head")
        f_out = sem("f_out")

        PAR_LOADS = 5 * T
        BIAS_LOADS = BJ * T

        block = ctx.enter_context(nc.Block())

        @block.sync
        def _(sp):
            def value(v):
                return v if isinstance(v, int) else sp.snap(sp.to_reg(v))

            def load_block(b, k, p, waits):
                n = value(b * BLOCK)
                waits = waits and [value(v) for v in waits]
                if waits:
                    sp.wait_ge(s_row_out[k], waits[0])
                    sp.wait_ge(s_z, waits[1])
                sp.dma_start(rows[0:p, k, :, 0:C], first_rows(x, n, p)).then_inc(s_row_in[k], 16)

            def store_block(b, k, p):
                n, done = value(b * BLOCK), value(b + 1)
                sp.wait_ge(s_rows_full, done)
                sp.wait_ge(s_row_oh, done)
                sp.dma_start(first_rows(node_rows, n, p), rows[0:p, k, :, :]).then_inc(s_row_out[k], 16)
                sp.wait_ge(s_norm, done)
                sp.dma_start(first_rows(out, n, p), z[0:p, k, :, :]).then_inc(s_out[k], 16)

            sp.wait_ge(s_pad, 1)
            flat = src[0:FULL_LANES * LANE_EDGES].rearrange("(p j) -> p j", j=LANE_EDGES)
            sp.dma_start(src_idx[0:112, :], flat[0:112, :]).then_inc(s_src, 16)
            sp.dma_start(src_idx[112:FULL_LANES, :], flat[112:FULL_LANES, :]).then_inc(s_src, 16)
            sp.dma_start(src_idx[FULL_LANES:P, 0:LAST_LANE],
                         src[FULL_LANES * LANE_EDGES:E].rearrange("(a j) -> a j", a=1)).then_inc(s_src, 16)
            for t, (W, a_s, a_d, We, a_e, b) in enumerate(convs):
                sp.dma_start(W3[:, t, :], W).then_inc(s_par, 16)
                sp.dma_start(We3[:, t, :], We).then_inc(s_par, 16)
                for col, a in ((a_src, a_s), (a_dst, a_d), (a_edge, a_e)):
                    sp.dma_start(col[:, t:t + 1], a.rearrange("(c a) -> c a", a=1)).then_inc(s_par, 16)
            for b in range(SLOTS - 1):
                load_block(b, b, P, None)
            sp.wait_ge(s_pad, 5)
            sp.dma_start(types[:, 0:FULL_BLOCKS, :],
                         node_type[0:FULL_BLOCKS * BLOCK].rearrange("(b p j) -> p b j", p=P, j=BJ))\
                .then_inc(s_types, 16)
            sp.dma_start(types[0:TAIL_P, FULL_BLOCKS, :],
                         node_type[FULL_BLOCKS * BLOCK:N].rearrange("(p j) -> p j", j=BJ)).then_inc(s_types, 16)
            for t, conv in enumerate(convs):
                for j in range(BJ):
                    sp.dma_start(bias_f[j * T + t:j * T + t + 1, j * C:(j + 1) * C],
                                 conv[5].rearrange("(a c) -> a c", a=1)).then_inc(s_bias, 16)

            sp.wait_ge(s_pad, 8)
            first = FULL_LANES * LANE_EDGES
            for buf, shift in ((dI, 0), (nI, 1), (pI, -1)):
                body = dst[max(shift, 0):][0:FULL_LANES * LANE_EDGES].rearrange("(p j) -> p j", j=LANE_EDGES)
                if shift >= 0:
                    sp.dma_start(buf[0:112, :], body[0:112, :]).then_inc(s_dst, 16)
                    sp.dma_start(buf[112:FULL_LANES, :], body[112:FULL_LANES, :]).then_inc(s_dst, 16)
                else:
                    sp.dma_start(buf[0:1, 1:LANE_EDGES],
                                 dst[0:LANE_EDGES - 1].rearrange("(a j) -> a j", a=1)).then_inc(s_dst, 16)
                    body = dst[LANE_EDGES - 1:first - 1].rearrange("(p j) -> p j", j=LANE_EDGES)
                    sp.dma_start(buf[1:FULL_LANES, :], body).then_inc(s_dst, 16)
                n = min(E, E - shift) - first if shift >= 0 else LAST_LANE + 1
                sp.dma_start(buf[FULL_LANES:P, 0:n],
                             dst[first + shift:first + shift + n].rearrange("(a j) -> a j", a=1))\
                    .then_inc(s_dst, 16)
            def step(b, i, k):
                ahead = b + SLOTS - 1
                ka = (k + SLOTS - 1) % SLOTS
                if k > 0 or not isinstance(b, int) or b > 0:
                    load_block(ahead, ka, P, (16 * (i + (0 if k == 0 else 1)), b))
                store_block(b, k, P)

            load_block(SLOTS - 1, SLOTS - 1, P, None)
            store_block(0, 0, P)
            for k in range(1, SLOTS):
                step(k, 0, k)
            with sp.Fori(1, BLOCK_LOOPS - 1) as i:
                for k in range(SLOTS):
                    step(SLOTS * i + k, i, k)
            for b in range(SLOTS * (BLOCK_LOOPS - 1), BLOCKS):
                k = b % SLOTS
                ahead = b + SLOTS - 1
                if ahead < BLOCKS:
                    load_block(ahead, ahead % SLOTS, P if ahead < FULL_BLOCKS else TAIL_P,
                               (16 * ((b - 1) // SLOTS + 1), b))
                store_block(b, k, P if b < FULL_BLOCKS else TAIL_P)

            kept = acc_rows.rearrange("(p j) c -> p j c", j=LANE_EDGES)

            def keep(g, q):
                j, done = value(U * g), value(U * g + U)
                sp.wait_ge(e_acc, done)
                sp.dma_start(kept[:, bass.ds(j, U), :], acc[:, q, :, :]).then_inc(s_keep[q], 16)

            for g in range(SLOTS):
                keep(g, g % 2)
            with sp.Fori(1, GROUPS // SLOTS) as i:
                for k in range(SLOTS):
                    keep(SLOTS * i + k, k % 2)
            for q in range(2):
                sp.wait_ge(s_keep[q], 16 * (GROUPS // 2))

        @block.gpsimd
        def _(pool):
            pool.memset(src_idx[:, :], 0).then_inc(s_pad, 1)
            pool.memset(ident[:, :], 0.0).then_inc(s_const, 1)
            for v in (types[:, :, :], z[0:BJ * T, 0, :, :], onehot3[:, :, :, :], bias_parts[:, :]):
                pool.memset(v, 0).then_inc(s_pad, 1)
            pool.wait_ge(s_const, 1)
            pool.affine_select(out=ident[:, :], in_=ident[:, :], compare_op=ALU.not_equal, fill=1.0,
                               base=0, pattern=[[-1, P]], channel_multiplier=1).then_inc(s_const, 1)
            pool.memset(ones[:, :], 1.0).then_inc(s_const, 1)
            pool.iota(lane_base[:, :], [[0, 1]], base=-1, channel_multiplier=LANE_EDGES).then_inc(s_const, 1)
            for buf in (dI, nI, pI):
                pool.memset(buf, PAD_DST).then_inc(s_pad, 1)

            def edge_scores():
                full = edge_attr[0:FULL_LANES * LANE_EDGES, :].rearrange("(p j) d -> p j d", j=LANE_EDGES)
                pool.wait_ge(s_idx, 1)
                pool.wait_ge(s_setC, 2)
                pool.memset(attr_c, 0.0).then_inc(s_score, 1)
                done, loads = 1, 0
                for c in range(4):
                    pool.wait_ge(s_score, done)
                    lo, hi = c * ATTR_CHUNK, (c + 1) * ATTR_CHUNK
                    pool.dma_start(attr_c[0:112], full[0:112, lo:hi, :]).then_inc(s_attr, 16)
                    pool.dma_start(attr_c[112:FULL_LANES], full[112:FULL_LANES, lo:hi, :]).then_inc(s_attr, 16)
                    loads += 2
                    n = min(hi, LAST_LANE) - lo
                    if n > 0:
                        e = FULL_LANES * LANE_EDGES + lo
                        pool.dma_start(attr_c[FULL_LANES:P, 0:n, :],
                                       edge_attr[e:e + n, :].rearrange("(a j) d -> a j d", a=1)).then_inc(s_attr, 16)
                        loads += 1
                    pool.wait_ge(s_attr, 16 * loads)
                    for t in range(T):
                        pool.tensor_tensor(attr_prod, attr_c, g_edge[:, t, :].unsqueeze(1)
                                           .to_broadcast([P, ATTR_CHUNK, ED]), ALU.mult).then_inc(s_score, 1)
                        done += 1
                        pool.wait_ge(s_score, done)
                        half = ED // 2
                        while half:
                            into = attr_prod[:, :, 0:half] if half > 1 else edge_score[:, lo:hi, t:t + 1]
                            pool.tensor_tensor(into, attr_prod[:, :, 0:half], attr_prod[:, :, half:2 * half],
                                               ALU.add).then_inc(s_score, 1)
                            done += 1
                            pool.wait_ge(s_score, done)
                            half //= 2

            def gather(idx, j, into, table, done):
                pool.indirect_dma_start(out=into, out_offset=None, in_=table, in_offset=bass.IndirectOffsetOnAxis(
                    ap=idx[:, j:j + 1], axis=0)).then_inc(done, 16)

            def gather_src(g):
                if g >= RING:
                    pool.wait_ge(s_staged, g - RING + 1)
                for u in range(U):
                    gather(src_idx, g * U + u, xs_ring[:, g % RING, u * C:(u + 1) * C], x, s_gx[g % SLOTS])

            def announce_src(g):
                pool.wait_ge(s_gx[g % SLOTS], 16 * U * (g // SLOTS + 1))
                pool.sem_inc(s_xs, 1)

            def gather_rows(g):
                if g >= SLOTS:
                    pool.wait_ge(e_z, g - SLOTS + 1)
                for u in range(U):
                    gather(row_idx, g * U + u, rows[:, g % SLOTS, u, :], node_rows, s_gr[g % SLOTS])

            def scatter_out(g):
                pool.wait_ge(e_norm, g + 1)
                for u in range(U):
                    j = g * U + u
                    pool.indirect_dma_start(
                        out=out, out_offset=bass.IndirectOffsetOnAxis(ap=out_idx[:, j:j + 1], axis=0),
                        in_=z[:, g % SLOTS, u, :], in_offset=None,
                        bounds_check=N - 1, oob_is_err=False).then_inc(s_sc[g % SLOTS], 16)

            pool.wait_ge(s_src, 48)
            for g in range(RING):
                gather_src(g)
                if g >= 2:
                    announce_src(g - 2)
            edge_scores()
            for k in range(SLOTS):
                pool.wait_ge(s_row_out[k], 16 * ((BLOCKS - 1 - k) // SLOTS + 1))
                pool.wait_ge(s_out[k], 16 * ((BLOCKS - 1 - k) // SLOTS + 1))
            pool.wait_ge(s_z, BLOCKS)
            pool.wait_ge(s_idx, 1)
            for g in range(GROUPS + LAG):
                if g < GROUPS:
                    gather_rows(g)
                if RING - 2 <= g + RING - 2 < GROUPS:
                    announce_src(g + RING - 2)
                if g + RING < GROUPS:
                    gather_src(g + RING)
                if g >= LAG:
                    scatter_out(g - LAG)
            pool.wait_ge(e_z, GROUPS)
            gather(row_idx, 0, rows[:, 0, 0, :], node_rows, f_rows)
            for q in range(2):
                pool.wait_ge(s_keep[q], 16 * (GROUPS // 2))
            gather(head_idx, 0, head_acc[:, :], acc_rows, f_head)
            for k in range(SLOTS):
                pool.wait_ge(s_sc[k], 16 * U * (GROUPS // SLOTS))
            pool.wait_ge(f_act, 5)
            pool.indirect_dma_start(
                out=out, out_offset=bass.IndirectOffsetOnAxis(ap=fix_idx[:, 0:1], axis=0),
                in_=z[:, 0, 0, :], in_offset=None, bounds_check=N - 1, oob_is_err=False).then_inc(f_out, 16)
            pool.wait_ge(f_out, 16)

        @block.tensor
        def _(pe):
            def transpose(o, i, n, eye=ident):
                return nc.tensor.transpose(o, i, eye[0:n, 0:n])

            pe.wait_ge(s_const, 3)
            pe.wait_ge(s_par, 16 * PAR_LOADS)
            for t in range(T):
                transpose(ps_x[0][:, t * C:(t + 1) * C], W3[:, t, :], P)
            for t in range(T):
                last = transpose(ps_x[1][:, t * ED:(t + 1) * ED], We3[:, t, :], ED)
            last.then_inc(s_setT, 1)
            pe.wait_ge(s_setC, 1)
            for t in range(T):
                nc.tensor.matmul(ps_a[:, t:t + 1], lhsT=WT[:, t, :], rhs=a_src[:, t:t + 1], start=True, stop=True)
                nc.tensor.matmul(ps_a[:, T + t:T + t + 1], lhsT=WT[:, t, :], rhs=a_dst[:, t:t + 1],
                                 start=True, stop=True)
                last = nc.tensor.matmul(ps_a[:, 64 + t * ED:64 + (t + 1) * ED], lhsT=a_edge_bc[:, t, :],
                                        rhs=WeT[:, t, :], start=True, stop=True)
            last.then_inc(s_setT, 1)
            pe.wait_ge(s_setC, 2)

            pe.wait_ge(s_onehots, 1)

            def node_block(b, i, k, p):
                q = k % 2
                pe.wait_ge(s_rep, b + 1)
                pe.wait_ge(s_ohT, b)
                transpose(ps_o[0:T * REP, 0:p], onehot3[0:p, q, :, :].rearrange("p r n -> p (r n)"), p, ident_b)\
                    .then_inc(s_ohT_ps, 1)
                pe.wait_ge(s_row_in[k], 16 * (i + 1))
                pe.wait_ge(s_xT, 2 * b)
                for h in range(2):
                    for j in range(4 * h, 4 * h + 4):
                        last = transpose(ps_x[h][:, (j % 4) * P:(j % 4) * P + p], rows[0:p, k, j, 0:C], p)
                    last.then_inc(s_xT_ps, 1)
                pe.wait_ge(s_ohT, b + 1)
                pe.wait_ge(s_bsel_used, 2 * b)
                for h in range(2):
                    nc.tensor.matmul(ps_b[h][0:p, :], lhsT=onehotT[:, q, 0:p],
                                     rhs=bias_parts[:, h * 4 * C:(h + 1) * 4 * C], start=True, stop=True)\
                        .then_inc(s_bsel, 1)
                pe.wait_ge(s_xT, 2 * b + 2)
                pe.wait_ge(s_al_used, back(b, 1))
                for j in range(BJ):
                    last = nc.tensor.matmul(ps_w[q][0:p, j * T:(j + 1) * T],
                                            lhsT=xT[:, q, j * P:j * P + p], rhs=V_dst[:, :],
                                            start=True, stop=True)
                last.then_inc(s_al, 1)

            for b in range(SLOTS):
                node_block(b, 0, b, P)
            with pe.Fori(1, BLOCK_LOOPS) as i:
                for k in range(SLOTS):
                    node_block(SLOTS * i + k, i, k, P)
            for b in range(SLOTS * BLOCK_LOOPS, BLOCKS):
                node_block(b, b // SLOTS, b % SLOTS, P if b < FULL_BLOCKS else TAIL_P)

            pe.wait_ge(s_ohT, BLOCKS)
            pe.wait_ge(s_al_used, BLOCKS)
            pe.wait_ge(s_bsel_used, 2 * BLOCKS)

            def source_scores(g, i, k):
                q = k % 2
                pe.wait_ge(s_staged, g + 1)
                pe.wait_ge(e_accT, back(2 * g, 2))
                for h, (lo, hi) in enumerate(((0, 4), (4, U))):
                    for u in range(lo, hi):
                        last = transpose(ps_x[h][:, (u - lo) * P:(u - lo + 1) * P], xst[:, q, u, :], P)
                    last.then_inc(e_xT_ps, 1)
                pe.wait_ge(e_rep, g + 1)
                pe.wait_ge(e_ohT, g)
                transpose(ps_o[0:T * REP, 0:P], onehot3[:, q, :, :].rearrange("p r n -> p (r n)"), P, ident_b)\
                    .then_inc(e_ohT_ps, 1)
                pe.wait_ge(e_xT, 2 * g + 2)
                pe.wait_ge(e_al_used, g)
                for u in range(U):
                    last = nc.tensor.matmul(ps_a[:, u * T:(u + 1) * T], lhsT=xT[:, q, u * P:(u + 1) * P],
                                            rhs=V_src[:, :], start=True, stop=True)
                last.then_inc(e_al, 1)

            def sums_transposed(g, k):
                q = k % 2
                pe.wait_ge(e_xT, 2 * g + 4 if not isinstance(g, int) else min(2 * g + 4, 2 * GROUPS))
                for h, (lo, hi) in enumerate(((0, 4), (4, U))):
                    pe.wait_ge(e_acc, U * g + hi)
                    for u in range(lo, hi):
                        last = transpose(ps_x[h][:, (u - lo) * P:(u - lo + 1) * P], acc[:, q, u, :], P)
                    last.then_inc(e_accT_ps, 1)

            def apply_w(g, k, tiles):
                q = k % 2
                pe.wait_ge(e_accT, 2 * g + 2)
                for u in tiles:
                    if u >= 4:
                        pe.wait_ge(e_w_used, U * g + u - 3)
                    elif u < 2:
                        pe.wait_ge(e_w_used, back(U * g, 2 - u))
                    else:
                        pe.wait_ge(e_bsel_used, 2 * g + u - 1)
                    nc.tensor.matmul(banks[u % 4][:, 0:T * C], lhsT=accT[:, q, u * P:(u + 1) * P],
                                     rhs=W3[:, :, :].rearrange("p t c -> p (t c)"), start=True, stop=True)\
                        .then_inc(e_w, 1)

            def biases(g, k):
                pe.wait_ge(e_ohT, g + 1)
                pe.wait_ge(e_w_used, U * g)
                for h, (lo, hi) in enumerate(((0, 4), (4, U))):
                    nc.tensor.matmul(ps_b[h][:, 0:(hi - lo) * C], lhsT=onehotT[:, k % 2, :],
                                     rhs=bias_parts[:, lo * C:hi * C], start=True, stop=True).then_inc(e_bsel, 1)

            def edge_step(g, i, k):
                if not isinstance(g, int) or g < GROUPS:
                    sums_transposed(g, k)
                if not isinstance(g, int) or g > 0:
                    apply_w(g - 1, k - 1, (4, 5, 6))
                if not isinstance(g, int) or g < GROUPS:
                    biases(g, k)
                    apply_w(g, k, (0, 1))
                    if not isinstance(g, int) or g + 2 < GROUPS:
                        source_scores(g + 2, i + (1 if k >= 2 else 0), (k + 2) % SLOTS)
                    apply_w(g, k, (2, 3))

            source_scores(0, 0, 0)
            source_scores(1, 0, 1)
            for g in range(SLOTS):
                edge_step(g, 0, g)
            with pe.Fori(1, GROUPS // SLOTS - 1) as i:
                for k in range(SLOTS):
                    edge_step(SLOTS * i + k, i, k)
            for g in range(GROUPS - SLOTS, GROUPS + 1):
                edge_step(g, g // SLOTS, g % SLOTS)

            pe.wait_ge(f_dve, 1)
            for c in range(5):
                last = transpose(ps_x[c // 4][0:1, (c % 4) * P:(c % 4 + 1) * P], cols[:, c:c + 1], P)
            last.then_inc(f_pe, 1)
            transpose(ps_w[0][:, 0:P], acc[:, (GROUPS - 1) % 2, U - 1, :], P)
            pe.wait_ge(f_head, 16)
            transpose(ps_w[0][:, P:2 * P], head_acc[:, :], P).then_inc(f_pe, 1)
            pe.wait_ge(f_dve, 3)
            nc.tensor.matmul(ps_b[0][:, :], lhsT=ones[0:1, :], rhs=xT[0:1, 1, 0:4 * P], start=True, stop=True)
            nc.tensor.matmul(ps_b[1][:, 0:1], lhsT=xT[0:1, 1, 4 * P:5 * P], rhs=ones[0:1, 0:1],
                             start=True, stop=True).then_inc(f_pe, 1)
            pe.wait_ge(f_rows, 16)
            pe.wait_ge(f_act, 2)
            transpose(ps_o[0:T * REP, 0:P], onehot3[:, 0, :, :].rearrange("p r n -> p (r n)"), P, ident_b)\
                .then_inc(f_pe, 1)
            pe.wait_ge(f_dve, 4)
            nc.tensor.matmul(ps_w[1][:, 0:T * C], lhsT=accT[:, 0, 0:P], rhs=W3[:, :, :].rearrange("p t c -> p (t c)"),
                             start=True, stop=True).then_inc(f_pe, 1)
            pe.wait_ge(f_act, 3)
            nc.tensor.matmul(ps_a[:, 0:C], lhsT=onehotT[:, 0, :], rhs=bias_parts[:, 0:C],
                             start=True, stop=True).then_inc(f_pe, 1)

        @block.scalar
        def _(act):
            def copy(o, i):
                return nc.scalar.activation(o, i, ACT.Copy)

            def normalise(zz, q, first, n, p, done):
                for j in range(n):
                    last = nc.scalar.activation(zz[0:p, j, :], zz[0:p, j, :], ACT.Identity,
                                                bias=nbias[0:p, q, first + j:first + j + 1],
                                                scale=rstd[0:p, q, first + j:first + j + 1])
                last.then_inc(done, 1)

            act.wait_ge(s_setC, 2)

            act.wait_ge(s_onehots, 1)

            def types_out(b, i, k, p):
                q = k % 2
                act.wait_ge(s_row_out[k], 16 * i)
                act.wait_ge(s_ohT_ps, back(b, 1))
                copy(onehot3[0:p, q, :, 0:BJ * T], onehot_all[0:p, b, :, :].rearrange("p j t -> p (j t)")
                     .unsqueeze(1).to_broadcast([p, 3, BJ * T])).then_inc(s_rep, 1)
                copy(rows[0:p, k, :, C + 1:ROW], onehot_all[0:p, b, :, :]).then_inc(s_row_oh, 1)
                act.wait_ge(s_ohT_ps, b + 1)
                act.wait_ge(s_bsel, back(2 * b, 2))
                copy(onehotT[:, q, 0:p], ps_o[0:T * REP, 0:p]).then_inc(s_ohT, 1)

            def transposes_out(b, k, p):
                q = k % 2
                act.wait_ge(s_al, back(b, 1))
                for h in range(2):
                    act.wait_ge(s_xT_ps, 2 * b + h + 1)
                    copy(xT[:, q, h * 512:(h + 1) * 512].rearrange("c (j p) -> c j p", p=P)[:, :, 0:p],
                         ps_x[h][:, :].rearrange("c (j p) -> c j p", p=P)[:, :, 0:p]).then_inc(s_xT, 1)

            def deviations(m, q):
                act.wait_ge(s_var, m + 1)
                nc.scalar.activation(std[:, q, :], st[:, q, 4, :], ACT.Sqrt, bias=eps[:, :]).then_inc(s_std, 1)

            def layer_norm(b, m, k, p):
                act.wait_ge(s_norm_par, m + 1)
                normalise(z[:, k], (k // 2) % 2, BJ * (k % 2), BJ, p, s_norm)

            def size(b):
                return P if not isinstance(b, int) or b < FULL_BLOCKS else TAIL_P

            def pair(m, i, k, before, now=True):
                if now:
                    for d in range(2):
                        types_out(2 * m + d, i, k + d, size(2 * m + d))
                        transposes_out(2 * m + d, k + d, size(2 * m + d))
                        if before:
                            if d == 0:
                                deviations(m - 1, (k // 2 + 1) % 2)
                            layer_norm(2 * m - 2 + d, m - 1, (k + 2 + d) % SLOTS, P)
                else:
                    deviations(m - 1, (k // 2 + 1) % 2)
                    for d in range(2):
                        layer_norm(2 * m - 2 + d, m - 1, (k + 2 + d) % SLOTS, size(2 * m - 2 + d))

            pair(0, 0, 0, False)
            pair(1, 0, 2, True)
            with act.Fori(1, BLOCK_LOOPS) as i:
                pair(2 * i, i, 0, True)
                pair(2 * i + 1, i, 2, True)
            pair(2 * BLOCK_LOOPS, BLOCK_LOOPS, 0, True)
            pair(2 * BLOCK_LOOPS + 1, BLOCK_LOOPS, 2, True, now=False)

            act.wait_ge(s_idx, 1)
            act.wait_ge(s_al, BLOCKS)
            act.wait_ge(s_bsel, 2 * BLOCKS)
            for k in range(SLOTS):
                act.wait_ge(s_out[k], 16 * ((BLOCKS - 1 - k) // SLOTS + 1))

            def stage(g, slot, k):
                act.wait_ge(s_xs, g + 1)
                act.wait_ge(e_xT_ps, back(2 * g, 2))
                act.wait_ge(e_px, back(U * g, U))
                copy(xst[:, k % 2, :, :].rearrange("p u c -> p (u c)"), xs_ring[:, slot, :]).then_inc(s_staged, 1)

            def source_out(g, i, k):
                q = k % 2
                act.wait_ge(s_gr[k], 16 * U * (i + 1))
                copy(onehot3[:, q, :, 0:U * T].rearrange("p r (j t) -> p r j t", t=T),
                     rows[:, k, 0:U, C + 1:ROW].unsqueeze(1).to_broadcast([P, 3, U, T])).then_inc(e_rep, 1)
                act.wait_ge(e_al, back(g, 1))
                for h, (lo, hi) in enumerate(((0, 4), (4, U))):
                    act.wait_ge(e_xT_ps, 2 * g + h + 1)
                    copy(xT[:, q, lo * P:hi * P], ps_x[h][:, 0:(hi - lo) * P]).then_inc(e_xT, 1)
                act.wait_ge(e_ohT_ps, g + 1)
                act.wait_ge(e_bsel, back(2 * g, 2))
                copy(onehotT[:, q, :], ps_o[0:T * REP, 0:P]).then_inc(e_ohT, 1)

            def acc_out(g, k):
                for h, (lo, hi) in enumerate(((0, 4), (4, U))):
                    act.wait_ge(e_accT_ps, 2 * g + h + 1)
                    if h == 0:
                        act.wait_ge(e_w, back(U * g, U))
                    copy(accT[:, k % 2, lo * P:hi * P], ps_x[h][:, 0:(hi - lo) * P]).then_inc(e_accT, 1)

            def weights(g, k):
                q = k % 2
                act.wait_ge(e_expo, g + 1)
                nc.scalar.activation(fp[:, q, :, :], expo[:, q, :, :], ACT.Exp).then_inc(e_exp, 1)
                act.wait_ge(e_exp, g + 1)
                act.wait_ge(e_acc, U * g)
                for u in range(U):
                    nc.scalar.activation(px[:, u, :], xst[:, q, u, :], ACT.Copy,
                                         scale=fp[:, q, 1, u:u + 1]).then_inc(e_px, 1)

            def edge_std(g, k):
                act.wait_ge(e_var, g + 1)
                nc.scalar.activation(std[:, k % 2, 0:U], st[:, k % 2, 4, 0:U], ACT.Sqrt, bias=eps[:, :])\
                    .then_inc(e_std, 1)

            def edge_norm(g, k):
                act.wait_ge(e_norm_par, g + 1)
                normalise(z[:, k], k % 2, 0, U, P, e_norm)

            def edge_step(g, i, k):
                known = isinstance(g, int)
                if not known or g + 2 < GROUPS:
                    stage(g + 2, (g + 2) % RING, (k + 2) % SLOTS)
                if not known or g < GROUPS:
                    acc_out(g, k)
                if not known or g >= 2:
                    edge_norm(g - 2, (k + 2) % SLOTS)
                if not known or g + 1 < GROUPS:
                    weights(g + 1, (k + 1) % SLOTS)
                if not known or g + 2 < GROUPS:
                    source_out(g + 2, i + (1 if k >= 2 else 0), (k + 2) % SLOTS)
                if not known or 1 <= g <= GROUPS:
                    edge_std(g - 1, (k + 3) % SLOTS)

            stage(0, 0, 0)
            source_out(0, 0, 0)
            stage(1, 1, 1)
            source_out(1, 0, 1)
            weights(0, 0)
            for g in range(SLOTS):
                edge_step(g, 0, g)
            with act.Fori(1, GROUPS // SLOTS - 1) as i:
                for k in range(SLOTS):
                    edge_step(SLOTS * i + k, i, k)
            for g in range(GROUPS - SLOTS, GROUPS + 2):
                edge_step(g, g // SLOTS, g % SLOTS)

            act.wait_ge(f_dve, 2)
            nc.scalar.activation(xT[0:1, 1, 0:4 * P], xT[0:1, 0, 0:4 * P], ACT.Exp).then_inc(f_act, 1)
            act.wait_ge(f_rows, 16)
            copy(onehot3[:, 0, :, 0:T], rows[:, 0, 0:1, C + 1:ROW].to_broadcast([P, 3, T])).then_inc(f_act, 1)
            act.wait_ge(f_pe, 4)
            copy(onehotT[:, 0, :], ps_o[0:T * REP, 0:P]).then_inc(f_act, 1)
            act.wait_ge(f_dve, 5)
            nc.scalar.activation(std[:, 0, 0:1], st[:, 0, 4, 0:1], ACT.Sqrt, bias=eps[:, :]).then_inc(f_act, 1)
            act.wait_ge(f_dve, 6)
            act.wait_ge(s_sc[0], 16 * U * (GROUPS // SLOTS))
            normalise(z[:, 0], 0, 0, 1, P, f_act)

        @block.vector
        def _(dve):
            tt = nc.vector.tensor_tensor
            ts = nc.vector.tensor_scalar
            stt = nc.vector.scalar_tensor_tensor

            class Order:

                def __init__(self, sem, base, total=None):
                    self.sem, self.base, self.total, self.n = sem, base, total, 0

                def done(self, instruction):
                    instruction.then_inc(self.sem, 1)
                    self.n += 1
                    return self.base + self.n

                def wait(self):
                    dve.wait_ge(self.sem, self.base + self.n)

                def link(self, instruction):
                    self.done(instruction)
                    self.wait()

                def end(self):
                    assert self.total in (None, self.n), self.n

            o = Order(s_dve_setup, 0)
            for v, value in ((eps[:, :], EPS), (M_all[:, 0:1], -BIG), (S_all[:, 0:1], 0.0),
                             (stats[:, :, :, :], 0.0)):
                o.done(nc.vector.memset(v, value))
            dve.wait_ge(s_const, 4)
            dve.wait_ge(s_par, 16 * PAR_LOADS)
            for t in range(T):
                o.done(ts(a_edge_bc[:, t, :], ones[:, :], a_edge[:, t:t + 1], None, ALU.mult))
            dve.wait_ge(s_setT, 1)
            o.done(nc.vector.tensor_copy(WT[:, :, :].rearrange("p t c -> p (t c)"), ps_x[0][:, 0:T * C]))
            o.wait()
            nc.vector.tensor_copy(WeT[:, :, :].rearrange("p t c -> p (t c)"), ps_x[1][:, 0:T * ED])\
                .then_inc(s_setC, 1)
            dve.wait_ge(s_setT, 2)
            o.done(nc.vector.tensor_copy(V_src[:, :], ps_a[:, 0:T]))
            o.done(nc.vector.tensor_copy(V_dst[:, :], ps_a[:, T:2 * T]))
            o.wait()
            nc.vector.tensor_copy(g_edge[:, :, :].rearrange("p t c -> p (t c)"), ps_a[:, 64:64 + T * ED])\
                .then_inc(s_setC, 1)
            dve.wait_ge(s_setC, 2)

            part = lambda r: bias_parts[r * REP:r * REP + BJ * T, :]
            o.link(nc.vector.tensor_copy(ident_b[:, :], ident[:, :]))
            dve.wait_ge(s_bias, 16 * BIAS_LOADS)
            o.link(nc.vector.tensor_copy(part(0), bias_f))
            o.link(tt(bias_r, bias_f, part(0), ALU.subtract))
            o.done(nc.vector.tensor_copy(part(1), bias_r))
            o.link(nc.vector.tensor_copy(bias_m, bias_r))
            o.link(tt(bias_r, bias_r, bias_m, ALU.subtract))
            o.link(nc.vector.tensor_copy(part(2), bias_r))
            dve.wait_ge(s_types, 32)
            one = lambda t: onehot_all[:, :, :, t]
            o.done(ts(one(0), types[:, :, :], 0.0, None, ALU.is_equal))
            o.done(ts(one(1), types[:, :, :], 1.0, None, ALU.is_equal))
            o.wait()
            o.link(tt(one(2), one(0), one(1), ALU.add))
            ts(one(2), one(2), -1.0, 1.0, ALU.mult, ALU.add).then_inc(s_onehots, 1)

            dve.wait_ge(s_dst, 16 * 9)
            for f, i in ((dF, dI), (nF, nI), (pF, pI)):
                o.done(nc.vector.tensor_copy(f, i))
            o.wait()
            last = LANE_EDGES - 1
            carries, inner, ends_here, fix = (cin[:, c:c + 1] for c in range(4))
            o.done(ts(hd, dF, dF[:, 0:1], None, ALU.is_equal))
            o.done(tt(carries, pF[:, 0:1], dF[:, 0:1], ALU.is_equal))
            o.done(tt(restart[:, :], pF, dF, ALU.not_equal))
            o.wait()
            o.done(ts(restart[:, :], restart[:, :], -BIG, None, ALU.mult))
            o.done(tt(pF, nF, dF, ALU.not_equal))
            o.wait()
            o.done(nc.vector.memset(restart[:, 0:1], -BIG))
            o.done(tt(head_end[:, 0:last], hd[:, 0:last], pF[:, 0:last], ALU.mult))
            o.done(nc.vector.tensor_copy(head_end[:, last:], hd[:, last:]))
            o.done(nc.vector.tensor_reduce(rs[:, 0:1], hd, X_AXIS, ALU.add))
            o.done(tt(cols[:, 4:5], carries, hd[:, last:], ALU.mult))
            o.done(ts(nF, hd, carries, None, ALU.mult))
            o.done(ts(inner, pF[:, last:], -1.0, 1.0, ALU.mult, ALU.add))
            o.wait()
            o.done(tt(head_idx[:, :], lane_base[:, :], rs[:, 0:1], ALU.add))
            o.done(ts(nF, nF, -1.0, 1.0, ALU.mult, ALU.add))
            o.done(tt(inner, inner, hd[:, last:], ALU.mult))
            o.wait()
            o.done(tt(nF, nF, pF, ALU.mult))
            o.done(ts(ends_here, inner, -1.0, 1.0, ALU.mult, ALU.add))
            o.wait()
            o.done(ts(nF, nF, -float(SKIP), float(SKIP), ALU.mult, ALU.add))
            o.done(tt(fix, ends_here, carries, ALU.mult))
            o.wait()
            o.done(tt(out_idx[:, :], nF, dF, ALU.add))
            o.done(ts(fix, fix, -float(SKIP), float(SKIP), ALU.mult, ALU.add))
            o.done(ts(row_idx[:, :], dF, float(N - 1), None, ALU.min))
            o.wait()
            o.link(tt(fix_idx[:, :], fix, dF[:, 0:1], ALU.add))
            dve.sem_inc(s_idx, 1)

            def block_statistics(o, zz, q, first, n, p):
                for j in range(n):
                    o.done(nc.vector.bn_stats(stats[0:p, q, first + j, :], zz[0:p, j, :]))

            def variances(o, q, n, done):
                o.wait()
                f = lambda c: stats[:, q, 0:n, c]
                v = lambda c: st[:, q, c, 0:n]
                o.done(tt(v(1), f(1), f(4), ALU.subtract))
                o.done(tt(v(0), f(1), f(4), ALU.add))
                o.done(tt(v(2), f(2), f(5), ALU.add))
                o.wait()
                o.link(stt(v(3), v(1), 0.25, v(1), ALU.mult, ALU.mult))
                stt(v(4), v(2), 1.0 / C, v(3), ALU.mult, ALU.add).then_inc(done, 1)

            def norm_parameters(o, q, n, done):
                o.link(nc.vector.reciprocal(rstd[:, q, 0:n], std[:, q, 0:n]))
                stt(nbias[:, q, 0:n], st[:, q, 0, 0:n], -0.5, rstd[:, q, 0:n], ALU.mult, ALU.mult)\
                    .then_inc(done, 1)

            dve.wait_ge(s_onehots, 1)

            def node_z(o, b, i, k, p):
                dve.wait_ge(s_out[k], 16 * i)
                dve.wait_ge(s_row_in[k], 16 * (i + 1))
                for h in range(2):
                    dve.wait_ge(s_bsel, 2 * b + h + 1)
                    tt(z[0:p, k, 4 * h:4 * h + 4, :], ps_b[h][0:p, :].rearrange("p (j c) -> p j c", c=C),
                       rows[0:p, k, 4 * h:4 * h + 4, 0:C], ALU.add).then_inc(s_bsel_used, 1)
                dve.wait_ge(s_bsel_used, 2 * b + 2)
                stt(z[0:p, k, :, :], z[0:p, k, :, :], 0.0, rows[0:p, k, :, 0:C], ALU.max, ALU.add).then_inc(s_z, 1)

            def node_scores(m, i, k, sizes):
                o = Order(s_node_al, 0)
                for d, p in enumerate(sizes):
                    b = 2 * m + d
                    dve.wait_ge(s_al, b + 1)
                    tt(prod[0:p, d, :, :], ps_w[d][0:p, 0:BJ * T].rearrange("p (j t) -> p j t", t=T),
                       onehot_all[0:p, b, :, :], ALU.mult).then_inc(s_al_used, 1)
                for d, p in enumerate(sizes):
                    b = 2 * m + d
                    dve.wait_ge(s_al_used, b + 1)
                    dve.wait_ge(s_row_out[k + d], 16 * i)
                    nc.vector.tensor_reduce(rows[0:p, k + d, :, C], prod[0:p, d, :, :], X_AXIS, ALU.add)\
                        .then_inc(s_rows_full, 1)

            def node_norm(m, q):
                dve.wait_ge(s_std, m + 1)
                norm_parameters(Order(s_node_np, m, 1), q, 2 * BJ, s_norm_par)

            def node_pair(m, i, k, before, sizes=(P, P)):
                q = (k // 2) % 2
                o = Order(s_node_st, 20 * m, 20)
                for d, p in enumerate(sizes):
                    b = 2 * m + d
                    node_z(o, b, i, k + d, p)
                    if d == 0 and before:
                        node_norm(m - 1, 1 - q)
                    dve.wait_ge(s_z, b + 1)
                    block_statistics(o, z[:, k + d], q, BJ * d, BJ, p)
                node_scores(m, i, k, sizes)
                variances(o, q, 2 * BJ, s_var)
                o.end()

            node_pair(0, 0, 0, False)
            node_pair(1, 0, 2, True)
            with dve.Fori(1, BLOCK_LOOPS) as i:
                node_pair(2 * i, i, 0, True)
                node_pair(2 * i + 1, i, 2, True)
            node_pair(2 * BLOCK_LOOPS, BLOCK_LOOPS, 0, True, (P, TAIL_P))
            node_norm(2 * BLOCK_LOOPS, 0)

            dve.wait_ge(s_norm, BLOCKS)
            dve.wait_ge(s_score, 61)
            nc.vector.memset(acc[:, 1, U - 1, :], 0.0).then_inc(e_zero, 1)
            dve.wait_ge(e_zero, 1)

            def columns(t, g, n=U):
                return t[:, bass.ds(g * U, n)]

            def scores(g, i, k):
                q = k % 2
                o = Order(e_dve_a, 7 * g, 7)
                sc = score[:, q, 0:U]
                dve.wait_ge(s_gr[k], 16 * U * (i + 1))
                dve.wait_ge(e_al, g + 1)
                tt(prod[:, q, 0:U, :], ps_a[:, 0:U * T].rearrange("p (j t) -> p j t", t=T),
                   edge_score[:, bass.ds(g * U, U), :], ALU.add).then_inc(e_al_used, 1)
                dve.wait_ge(e_al_used, g + 1)
                o.link(tt(prod[:, q, 0:U, :], prod[:, q, 0:U, :], rows[:, k, 0:U, C + 1:ROW], ALU.mult))
                o.link(nc.vector.tensor_reduce(sc, prod[:, q, 0:U, :], X_AXIS, ALU.add))
                o.link(tt(sc, sc, rows[:, k, 0:U, C], ALU.add))
                o.link(stt(sc, sc, 0.2, sc, ALU.mult, ALU.max))
                M_new = M_all[:, bass.ds(g * U + 1, U)]
                o.link(nc.vector.tensor_tensor_scan(M_new, columns(restart, g), sc, columns(M_all, g, 1),
                                                    ALU.add, ALU.max))
                o.link(tt(expo[:, q, 0, :], columns(M_all, g), columns(restart, g), ALU.add))
                o.link(tt(expo[:, q, 0, :], expo[:, q, 0, :], M_new, ALU.subtract))
                o.end()
                tt(expo[:, q, 1, :], sc, M_new, ALU.subtract).then_inc(e_expo, 1)

            def accumulate(g, i, k):
                q = k % 2
                o = Order(e_dve_b, 4 * g, 4)
                dve.wait_ge(e_exp, g + 1)
                S_new = S_all[:, bass.ds(g * U + 1, U)]
                o.link(nc.vector.tensor_tensor_scan(S_new, fp[:, q, 0, :], fp[:, q, 1, :], columns(S_all, g, 1),
                                                    ALU.mult, ALU.add))
                dve.wait_ge(e_accT_ps, back(2 * g, 2))
                dve.wait_ge(s_keep[q], 16 * (2 * i + k // 2))
                for u in range(U):
                    before = acc[:, q, u - 1, :] if u else acc[:, 1 - q, U - 1, :]
                    dve.wait_ge(e_px, U * g + u + 1)
                    dve.wait_ge(e_acc, U * g + u)
                    stt(acc[:, q, u, :], before, fp[:, q, 0, u:u + 1], px[:, u, :], ALU.mult, ALU.add)\
                        .then_inc(e_acc, 1)
                o.link(ts(rs[:, 0:U], S_new, TINY, None, ALU.add))
                o.link(nc.vector.reciprocal(rs[:, 0:U], rs[:, 0:U]))
                o.link(tt(kk[:, q, :, :], rows[:, k, 0:U, C + 1:ROW],
                          rs[:, 0:U].unsqueeze(2).to_broadcast([P, U, T]), ALU.mult))
                o.end()

            def residuals(g, i, k):
                dve.wait_ge(s_sc[k], 16 * U * i)
                for h, (lo, hi) in enumerate(((0, 4), (4, U))):
                    dve.wait_ge(e_bsel, 2 * g + h + 1)
                    tt(z[:, k, lo:hi, :], ps_b[h][:, 0:(hi - lo) * C].rearrange("p (j c) -> p j c", c=C),
                       rows[:, k, lo:hi, 0:C], ALU.add).then_inc(e_bsel_used, 1)

            def outputs(g, k):
                q = k % 2
                dve.wait_ge(e_bsel_used, 2 * g + 2)
                o = Order(e_dve_c, 25 * g, 25)
                before = {}
                for us in ((0, 1), (2, 3), (4, 5), (6,)):
                    for t in range(T):
                        for u in us:
                            if t == 0:
                                dve.wait_ge(e_w, U * g + u + 1)
                            else:
                                dve.wait_ge(e_dve_c, before[u])
                            ins = stt(z[:, k, u, :], banks[u % 4][:, t * C:(t + 1) * C], kk[:, q, u, t:t + 1],
                                      z[:, k, u, :], ALU.mult, ALU.add)
                            if t < T - 1:
                                before[u] = o.done(ins)
                            else:
                                ins.then_inc(e_w_used, 1)
                dve.wait_ge(e_w_used, U * g + U)
                stt(z[:, k, 0:U, :], z[:, k, 0:U, :], 0.0, rows[:, k, 0:U, 0:C], ALU.max, ALU.add).then_inc(e_z, 1)
                dve.wait_ge(e_z, g + 1)
                block_statistics(o, z[:, k], q, 0, U, P)
                variances(o, q, U, e_var)
                o.end()

            def norms(g, k):
                dve.wait_ge(e_std, g + 1)
                norm_parameters(Order(e_dve_n, g, 1), k % 2, U, e_norm_par)

            def edge_step(g, i, k):
                known = isinstance(g, int)
                if not known or g < GROUPS:
                    accumulate(g, i, k)
                if not known or g >= 2:
                    norms(g - 2, (k + 2) % SLOTS)
                if not known or g + 1 < GROUPS:
                    scores(g + 1, i + (1 if k == SLOTS - 1 else 0), (k + 1) % SLOTS)
                if not known or g >= 1:
                    outputs(g - 1, (k + 3) % SLOTS)
                if not known or g < GROUPS:
                    residuals(g, i, k)

            scores(0, 0, 0)
            for g in range(SLOTS):
                edge_step(g, 0, g)
            with dve.Fori(1, GROUPS // SLOTS - 1) as i:
                for k in range(SLOTS):
                    edge_step(SLOTS * i + k, i, k)
            for g in range(GROUPS - SLOTS, GROUPS + 1):
                edge_step(g, g // SLOTS, g % SLOTS)
            norms(GROUPS - 1, SLOTS - 1)

            o = Order(s_dve_last, 0)
            dve.wait_ge(e_norm, GROUPS)
            dve.wait_ge(e_z, GROUPS)
            hM = px[:, 0:4, :].rearrange("p a c -> p (a c)")[:, 0:LANE_EDGES]
            for c, v in ((2, M_all), (3, S_all)):
                o.link(tt(hM, v[:, 1:], head_end[:, :], ALU.mult))
                o.link(nc.vector.tensor_reduce(cols[:, c:c + 1], hM, X_AXIS, ALU.add))
                o.link(nc.vector.tensor_copy(cols[:, c - 2:c - 1], v[:, LANE_EDGES:]))
            dve.sem_inc(f_dve, 1)

            row = z[0:1, 1, :, :].rearrange("p a c -> p (a c)")
            tailM, tailS, headM, headS, through = (row[:, c * P:(c + 1) * P] for c in range(5))
            Kbuf, Sbuf = xT[0:1, 0, 512:512 + P + 1], xT[0:1, 0, 704:704 + P + 1]
            headMx, headSx = row[:, 5 * P:6 * P], row[:, 6 * P:7 * P]
            factor = lambda j: xT[0:1, 0, j * P:(j + 1) * P]
            expd = lambda j: xT[0:1, 1, j * P:(j + 1) * P]
            dve.wait_ge(f_pe, 2)
            o.done(nc.vector.tensor_copy(row[:, 0:4 * P], ps_x[0][0:1, :]))
            o.done(ts(through, ps_x[1][0:1, 0:P], -1.0, BIG, ALU.add, ALU.mult))
            o.done(nc.vector.memset(Kbuf[:, 0:1], -BIG))
            o.done(nc.vector.memset(Sbuf[:, 0:1], 0.0))
            o.wait()
            o.link(nc.vector.tensor_tensor_scan(Kbuf[:, 1:], through, tailM, -BIG, ALU.add, ALU.max))
            o.link(tt(factor(0), Kbuf[:, 0:P], through, ALU.add))
            o.link(tt(factor(0), factor(0), Kbuf[:, 1:], ALU.subtract))
            o.link(tt(factor(1), tailM, Kbuf[:, 1:], ALU.subtract))
            o.link(tt(headMx, Kbuf[:, 0:P], headM, ALU.max))
            o.link(tt(factor(2), Kbuf[:, 0:P], headMx, ALU.subtract))
            o.link(tt(factor(3), headM, headMx, ALU.subtract))
            dve.sem_inc(f_dve, 1)
            dve.wait_ge(f_act, 1)
            o.link(tt(tailS, tailS, expd(1), ALU.mult))
            o.link(nc.vector.tensor_tensor_scan(Sbuf[:, 1:], expd(0), tailS, 0.0, ALU.mult, ALU.add))
            o.link(tt(headSx, Sbuf[:, 0:P], expd(2), ALU.mult))
            o.link(tt(headS, headS, expd(3), ALU.mult))
            o.link(tt(headS, headS, headSx, ALU.add))
            o.link(ts(headS, headS, TINY, None, ALU.add))
            o.link(nc.vector.reciprocal(expd(4), headS))
            dve.sem_inc(f_dve, 1)

            dve.wait_ge(f_pe, 3)
            bc = lambda j: xT[:, 0, j * P:(j + 1) * P]
            carry = px[:, 0:2, :].rearrange("p a c -> p (a c)")[:, 0:P + 1]
            whole = accT[:, 0, 0:P]
            o.done(nc.vector.tensor_copy(xT[:, 0, 0:4 * P], ps_b[0][:, :]))
            o.done(nc.vector.tensor_copy(rs[:, 0:1], ps_b[1][:, 0:1]))
            o.done(nc.vector.memset(carry[:, 0:1], 0.0))
            o.wait()
            o.link(tt(bc(1), ps_w[0][:, 0:P], bc(1), ALU.mult))
            o.link(nc.vector.tensor_tensor_scan(carry[:, 1:], bc(0), bc(1), 0.0, ALU.mult, ALU.add))
            o.link(tt(bc(3), ps_w[0][:, P:2 * P], bc(3), ALU.mult))
            o.link(tt(bc(2), carry[:, 0:P], bc(2), ALU.mult))
            o.link(tt(whole, bc(2), bc(3), ALU.add))
            dve.sem_inc(f_dve, 1)

            dve.wait_ge(f_rows, 16)
            o.link(ts(kk[:, 0, 0, :], rows[:, 0, 0, C + 1:ROW], rs[:, 0:1], None, ALU.mult))
            dve.wait_ge(f_pe, 6)
            o.link(tt(z[:, 0, 0, :], ps_a[:, 0:C], rows[:, 0, 0, 0:C], ALU.add))
            for t in range(T):
                o.link(stt(z[:, 0, 0, :], ps_w[1][:, t * C:(t + 1) * C], kk[:, 0, 0, t:t + 1], z[:, 0, 0, :],
                           ALU.mult, ALU.add))
            o.link(stt(z[:, 0, 0, :], z[:, 0, 0, :], 0.0, rows[:, 0, 0, 0:C], ALU.max, ALU.add))
            block_statistics(o, z[:, 0], 0, 0, 1, P)
            variances(o, 0, 1, f_dve)
            dve.wait_ge(f_act, 4)
            norm_parameters(o, 0, 1, f_dve)


_PARAMS = ("W", "as", "ad", "We", "ae", "b")


def kernel(**inputs):
    import numpy as np
    import concourse.bacc as bacc
    from concourse.bass_utils import run_bass_kernel_spmd

    nc = bacc.Bacc("TRN2", target_bir_lowering=False, num_devices=1)
    arrays = {}

    def given(name):
        a = np.ascontiguousarray(inputs[name])
        arrays[f"in_{name}_dram"] = a
        return nc.dram_tensor(f"in_{name}_dram", a.shape, mybir.dt.from_np(a.dtype), kind="ExternalInput").ap()

    graph = [given(name) for name in ("x", "src", "dst", "edge_attr_16", "node_type_3")]
    convs = [[given(f"L0_gnn_{p}{c}") for p in _PARAMS] for c in "vri"]
    shape = inputs["x"].shape
    out = nc.dram_tensor("out_0_dram", shape, mybir.dt.float32, kind="ExternalOutput").ap()
    gat_kernel(nc, *graph, convs, out)
    r = run_bass_kernel_spmd(nc, [arrays], core_ids=[0])
    return r.results[0]["out_0_dram"]
```

```python
import concourse.bass as bass
from concourse import mybir
from contextlib import ExitStack


def gat_kernel(nc, x, src, dst, edge_attr, node_type, convs, out):
    fp32 = mybir.dt.float32
    i32 = mybir.dt.int32
    bf16 = mybir.dt.bfloat16
    ALU = mybir.AluOpType
    ACT = mybir.ActivationFunctionType
    X_AXIS = mybir.AxisListType.X

    N, C = x.shape
    E, ED = edge_attr.shape
    P = 128
    T = 3
    BIG = 1.0e30
    EPS = 1e-5
    TINY = 1e-16

    BJ = 8
    BLOCK = P * BJ
    FULL_BLOCKS = N // BLOCK
    TAIL_P = (N - FULL_BLOCKS * BLOCK) // BJ
    BLOCKS = FULL_BLOCKS + 1
    assert FULL_BLOCKS * BLOCK + TAIL_P * BJ == N
    SLOTS = 4
    BLOCK_LOOPS = FULL_BLOCKS // SLOTS

    U = 7
    LANE_EDGES = -(-E // (P * U * SLOTS)) * U * SLOTS
    GROUPS = LANE_EDGES // U
    FULL_LANES = E // LANE_EDGES
    LAST_LANE = E - FULL_LANES * LANE_EDGES
    assert FULL_LANES == P - 1 and 1 < LAST_LANE < LANE_EDGES
    PAD_DST = 1 << 17
    SKIP = 1 << 18
    assert N < PAD_DST
    RING = 28
    DIRECT = SLOTS
    LATER = GROUPS - RING - DIRECT
    assert DIRECT == SLOTS and LATER == 4 * 6 and LATER % SLOTS == 0 and RING % SLOTS == 0
    ROW = C + T
    LAG = 5
    ATTR_CHUNK = LANE_EDGES // 4

    def back(count, n):
        return max(count - n, 0) if isinstance(count, int) else count - n

    node_rows = nc.dram_tensor("node_rows", (N, ROW), fp32).ap()
    acc_rows = nc.dram_tensor("acc_rows", (P * LANE_EDGES, C), fp32).ap()
    later_rows = nc.dram_tensor("later_rows", (P * LATER * U, C), fp32).ap()\
        .rearrange("(p n) c -> p n c", n=LATER * U)
    REP = 32

    def first_rows(t, n, p):
        return t[bass.ds(n, p * BJ), :].rearrange("(p j) c -> p j c", j=BJ)

    with ExitStack() as ctx:
        def sb(name, shape, dt=fp32):
            return ctx.enter_context(nc.sbuf_tensor(name, shape, dt))

        def pb(name, n=512, dt=fp32):
            return ctx.enter_context(nc.psum_tensor(name, [P, n], dt))

        def sem(name):
            return ctx.enter_context(nc.semaphore(name))

        ident = sb("ident", [P, P])
        ident_b = sb("ident_b", [P, P], bf16)
        ones = sb("ones", [P, P])
        W3 = sb("W3", [P, T, C])
        WT = sb("WT", [P, T, C])
        We3 = sb("We3", [ED, T, C])
        WeT = sb("WeT", [P, T, ED])
        a_src = sb("a_src", [P, T])
        a_dst = sb("a_dst", [P, T])
        a_edge = sb("a_edge", [P, T])
        a_edge_bc = sb("a_edge_bc", [P, T, P])
        V_src = sb("V_src", [P, T])
        V_dst = sb("V_dst", [P, T])
        g_edge = sb("g_edge", [P, T, ED])
        bias_parts = sb("bias_parts", [T * REP, BJ * C], bf16)
        src_idx = sb("src_idx", [P, LANE_EDGES], i32)
        row_idx = sb("row_idx", [P, LANE_EDGES], i32)
        out_idx = sb("out_idx", [P, LANE_EDGES], i32)
        fix_idx = sb("fix_idx", [P, 1], i32)
        restart = sb("restart", [P, LANE_EDGES])
        head_end = sb("head_end", [P, LANE_EDGES])
        edge_score = sb("edge_score", [P, LANE_EDGES, T])
        M_all = sb("M_all", [P, LANE_EDGES + 1])
        S_all = sb("S_all", [P, LANE_EDGES + 1])
        xs_ring = sb("xs_ring", [P, RING, U * C])
        rows = sb("rows", [P, SLOTS, BJ, ROW])
        z = sb("z", [P, SLOTS, BJ, C])
        xT = sb("xT", [P, 2, BJ * C])
        xdT = sb("xdT", [P, U * C])
        bias_rows = sb("bias_rows", [BJ * T, C])
        bias_split = sb("bias_split", [BJ * T, 3, C], bf16)
        own_j = sb("own_j", [BJ * T, BJ])
        onehot_all = sb("onehot_all", [P, BLOCKS, BJ * T], bf16)
        onehot3 = sb("onehot3", [P, 2, 3, REP], bf16)
        onehotT = sb("onehotT", [T * REP, 2, P], bf16)
        xst = sb("xst", [P, 2, U, C])
        px = sb("px", [P, U, C])
        acc = sb("acc", [P, 2, U, C])
        accT = sb("accT", [P, 2, U * C])
        head_acc = sb("head_acc", [P, C])
        prod = sb("prod", [P, 2, BJ, T])
        score = sb("score", [P, 2, BJ])
        expo = sb("expo", [P, 2, 2, U])
        fp = sb("fp", [P, 2, 2, U])
        rs = sb("rs", [P, BJ])
        kk = sb("kk", [P, 2, U, T])
        stats = sb("stats", [P, 2, 2 * BJ, 6])
        st = sb("st", [P, 2, 5, 2 * BJ])
        std = sb("std", [P, 2, 2 * BJ])
        rstd = sb("rstd", [P, 2, 2 * BJ])
        nbias = sb("nbias", [P, 2, 2 * BJ])
        lane_base = sb("lane_base", [P, 1], i32)
        head_idx = sb("head_idx", [P, 1], i32)
        eps = sb("eps", [P, 1])
        cols = sb("cols", [P, 6])
        cin = sb("cin", [P, 4])

        types = px[:, :, :].rearrange("p a c -> p (a c)")[:, 0:BLOCKS * BJ].bitcast(i32)\
            .rearrange("p (b j) -> p b j", j=BJ)
        dI = acc[:, 0, 0:4, :].rearrange("p a c -> p (a c)")[:, 0:LANE_EDGES].bitcast(i32)
        nI = acc[:, 1, 0:4, :].rearrange("p a c -> p (a c)")[:, 0:LANE_EDGES].bitcast(i32)
        pI = xst[:, 0, 0:4, :].rearrange("p a c -> p (a c)")[:, 0:LANE_EDGES].bitcast(i32)
        dF = xst[:, 1, 0:4, :].rearrange("p a c -> p (a c)")[:, 0:LANE_EDGES]
        nF = accT[:, 0, 0:LANE_EDGES]
        pF = accT[:, 1, 0:LANE_EDGES]
        hd = px[:, 0:4, :].rearrange("p a c -> p (a c)")[:, 0:LANE_EDGES]
        attr_c = acc[:, :, :, :].rearrange("p q u c -> p (q u c)")[:, 0:ATTR_CHUNK * ED]\
            .rearrange("p (j d) -> p j d", d=ED)
        attr_prod = accT[:, :, :].rearrange("p q n -> p (q n)")[:, 0:ATTR_CHUNK * ED]\
            .rearrange("p (j d) -> p j d", d=ED)

        ps_x = [pb("ps_x0"), pb("ps_x1")]
        ps_b = [pb("ps_b0"), pb("ps_b1")]
        ps_w = [pb("ps_w0"), pb("ps_w1")]
        banks = [*ps_w, *ps_b]
        ps_a = pb("ps_a")
        ps_o = pb("ps_o", 1024, bf16)

        s_const = sem("s_const")
        s_par = sem("s_par")
        s_bias = sem("s_bias")
        s_pad = sem("s_pad")
        s_src = sem("s_src")
        s_dst = sem("s_dst")
        s_types = sem("s_types")
        s_attr = sem("s_attr")
        s_score = sem("s_score")
        s_onehots = sem("s_onehots")
        s_keep = [sem(f"s_keep{q}") for q in range(2)]
        s_setT = sem("s_setT")
        s_setC = sem("s_setC")
        s_idx = sem("s_idx")
        s_row_in = [sem(f"s_row_in{k}") for k in range(SLOTS)]
        s_row_out = [sem(f"s_row_out{k}") for k in range(SLOTS)]
        s_out = [sem(f"s_out{k}") for k in range(SLOTS)]
        s_rep = sem("s_rep")
        s_row_oh = sem("s_row_oh")
        s_ohT_ps = sem("s_ohT_ps")
        s_ohT = sem("s_ohT")
        s_bsel = sem("s_bsel")
        s_bsel_used = sem("s_bsel_used")
        s_var = sem("s_var")
        s_std = sem("s_std")
        s_norm_par = sem("s_norm_par")
        s_norm = sem("s_norm")
        s_gx = [sem(f"s_gx{k}") for k in range(SLOTS)]
        s_gr = [sem(f"s_gr{k}") for k in range(SLOTS)]
        s_sc = [sem(f"s_sc{k}") for k in range(SLOTS)]
        s_later = sem("s_later")
        s_refill = [sem(f"s_refill{k}") for k in range(SLOTS)]
        s_xs = sem("s_xs")
        s_staged = sem("s_staged")
        e_xT_ps = sem("e_xT_ps")
        e_xT = sem("e_xT")
        e_xdT_ps = sem("e_xdT_ps")
        e_xdT = sem("e_xdT")
        e_al = sem("e_al")
        e_al_used = sem("e_al_used")
        e_rep = sem("e_rep")
        e_ohT_ps = sem("e_ohT_ps")
        e_ohT = sem("e_ohT")
        e_expo = sem("e_expo")
        e_exp = sem("e_exp")
        e_px = sem("e_px")
        e_acc = sem("e_acc")
        e_accT_ps = sem("e_accT_ps")
        e_accT = sem("e_accT")
        e_w = sem("e_w")
        e_w_used = sem("e_w_used")
        e_bsel = sem("e_bsel")
        e_bsel_used = sem("e_bsel_used")
        e_z = sem("e_z")
        e_var = sem("e_var")
        e_std = sem("e_std")
        e_norm_par = sem("e_norm_par")
        e_norm = sem("e_norm")
        s_dve_setup = sem("s_dve_setup")
        s_dve_par = sem("s_dve_par")
        s_dve_flags = sem("s_dve_flags")
        s_dve_states = sem("s_dve_states")
        s_node_st = sem("s_node_st")
        s_node_np = sem("s_node_np")
        e_zero = sem("e_zero")
        e_dve_a = sem("e_dve_a")
        e_dve_b = sem("e_dve_b")
        e_dve_c = sem("e_dve_c")
        e_dve_n = sem("e_dve_n")
        e_scan = sem("e_scan")
        s_dve_last = sem("s_dve_last")
        f_pe = sem("f_pe")
        f_dve = sem("f_dve")
        f_act = sem("f_act")
        f_rows = sem("f_rows")
        f_head = sem("f_head")
        f_out = sem("f_out")

        PAR_LOADS = 5 * T
        BIAS_LOADS = T

        block = ctx.enter_context(nc.Block())

        @block.sync
        def _(sp):
            def value(v):
                return v if isinstance(v, int) else sp.snap(sp.to_reg(v))

            def load_block(b, i, k, p):
                n = value(b * BLOCK)
                if not isinstance(i, int) or i > 0:
                    stored, read = value(16 * i), value(2 * (b - SLOTS + 1))
                    sp.wait_ge(s_row_out[k], stored)
                    sp.wait_ge(s_bsel_used, read)
                sp.dma_start(rows[0:p, k, :, 0:C], first_rows(x, n, p)).then_inc(s_row_in[k], 16)

            def store_rows(b, k, p):
                n, done = value(b * BLOCK), value(b + 1)
                sp.wait_ge(s_row_oh, done)
                sp.dma_start(first_rows(node_rows, n, p), rows[0:p, k, :, :]).then_inc(s_row_out[k], 16)

            def store_out(b, k, p):
                n, done = value(b * BLOCK), value(b + 1)
                sp.wait_ge(s_norm, done)
                sp.dma_start(first_rows(out, n, p), z[0:p, k, :, :]).then_inc(s_out[k], 16)

            sp.wait_ge(s_pad, 1)
            flat = src[0:FULL_LANES * LANE_EDGES].rearrange("(p j) -> p j", j=LANE_EDGES)
            sp.dma_start(src_idx[0:112, :], flat[0:112, :]).then_inc(s_src, 16)
            sp.dma_start(src_idx[112:FULL_LANES, :], flat[112:FULL_LANES, :]).then_inc(s_src, 16)
            sp.dma_start(src_idx[FULL_LANES:P, 0:LAST_LANE],
                         src[FULL_LANES * LANE_EDGES:E].rearrange("(a j) -> a j", a=1)).then_inc(s_src, 16)
            for t, conv in enumerate(convs):
                sp.dma_start(bias_rows[t::T, :], conv[5].rearrange("(a c) -> a c", a=1).to_broadcast([BJ, C]))\
                    .then_inc(s_bias, 16)
            sp.wait_ge(s_pad, 2)
            sp.dma_start(types[0:TAIL_P, FULL_BLOCKS, :],
                         node_type[FULL_BLOCKS * BLOCK:N].rearrange("(p j) -> p j", j=BJ)).then_inc(s_types, 16)
            sp.dma_start(types[:, 0:FULL_BLOCKS, :],
                         node_type[0:FULL_BLOCKS * BLOCK].rearrange("(b p j) -> p b j", p=P, j=BJ))\
                .then_inc(s_types, 16)
            for b in range(SLOTS):
                load_block(b, 0, b, P)
            for t, (W, a_s, a_d, We, a_e, b) in enumerate(convs):
                sp.dma_start(W3[:, t, :], W).then_inc(s_par, 16)
                sp.dma_start(We3[:, t, :], We).then_inc(s_par, 16)
                for col, a in ((a_src, a_s), (a_dst, a_d), (a_edge, a_e)):
                    sp.dma_start(col[:, t:t + 1], a.rearrange("(c a) -> c a", a=1)).then_inc(s_par, 16)

            sp.wait_ge(s_pad, 7)
            first = FULL_LANES * LANE_EDGES
            for buf, shift in ((dI, 0), (nI, 1), (pI, -1)):
                body = dst[max(shift, 0):][0:FULL_LANES * LANE_EDGES].rearrange("(p j) -> p j", j=LANE_EDGES)
                if shift >= 0:
                    sp.dma_start(buf[0:112, :], body[0:112, :]).then_inc(s_dst, 16)
                    sp.dma_start(buf[112:FULL_LANES, :], body[112:FULL_LANES, :]).then_inc(s_dst, 16)
                else:
                    sp.dma_start(buf[0:1, 1:LANE_EDGES],
                                 dst[0:LANE_EDGES - 1].rearrange("(a j) -> a j", a=1)).then_inc(s_dst, 16)
                    body = dst[LANE_EDGES - 1:first - 1].rearrange("(p j) -> p j", j=LANE_EDGES)
                    sp.dma_start(buf[1:FULL_LANES, :], body).then_inc(s_dst, 16)
                n = min(E, E - shift) - first if shift >= 0 else LAST_LANE + 1
                sp.dma_start(buf[FULL_LANES:P, 0:n],
                             dst[first + shift:first + shift + n].rearrange("(a j) -> a j", a=1))\
                    .then_inc(s_dst, 16)

            def size(b):
                return P if not isinstance(b, int) or b < FULL_BLOCKS else TAIL_P

            def node_step(b, i, k):
                known = isinstance(b, int)
                if (not known or b > 0) and (not known or b + 3 < BLOCKS):
                    load_block(b + 3, i + (1 if k > 0 else 0), (k + 3) % SLOTS, size(b + 3))
                if not known or b + 2 < BLOCKS:
                    store_rows(b + 2, (k + 2) % SLOTS, size(b + 2))
                if not known or b > 0:
                    store_out(b - 1, (k + 3) % SLOTS, size(b - 1))

            for b in range(2):
                store_rows(b, b, P)
            for b in range(SLOTS):
                node_step(b, 0, b)
            with sp.Fori(1, BLOCK_LOOPS - 1) as i:
                for k in range(SLOTS):
                    node_step(SLOTS * i + k, i, k)
            for b in range(SLOTS * (BLOCK_LOOPS - 1), BLOCKS + 1):
                node_step(b, b // SLOTS, b % SLOTS)

            kept = acc_rows.rearrange("(p j) c -> p j c", j=LANE_EDGES)

            def keep(g, q):
                j, done = value(U * g), value(U * g + U)
                sp.wait_ge(e_acc, done)
                sp.dma_start(kept[:, bass.ds(j, U), :], acc[:, q, :, :]).then_inc(s_keep[q], 16)

            def refill(g, k):
                slot, j, staged = value(g % RING), value(U * (g - DIRECT)), value(g + 1)
                sp.wait_ge(s_staged, staged)
                sp.dma_start(xs_ring[:, bass.ds(slot, 1), :],
                             later_rows[:, bass.ds(j, U), :].rearrange("p n c -> p (n c)").unsqueeze(1))\
                    .then_inc(s_refill[k], 16)

            def announce(i, k):
                landed = value(16 * i)
                sp.wait_ge(s_refill[k], landed)
                sp.sem_inc(s_xs, 1)

            for g in range(2 * SLOTS):
                if g >= DIRECT:
                    refill(g, g % SLOTS)
                keep(g, g % 2)
            with sp.Fori(2, LATER // SLOTS + 1) as i:
                for k in range(SLOTS):
                    announce(i - 1, k)
                    refill(SLOTS * i + k, k)
                    keep(SLOTS * i + k, k % 2)
            for k in range(SLOTS):
                announce(LATER // SLOTS, k)
            with sp.Fori(LATER // SLOTS + 1, GROUPS // SLOTS) as i:
                for k in range(SLOTS):
                    keep(SLOTS * i + k, k % 2)
            for q in range(2):
                sp.wait_ge(s_keep[q], 16 * (GROUPS // 2))

        @block.gpsimd
        def _(pool):
            pool.memset(src_idx[:, :], 0).then_inc(s_pad, 1)
            pool.memset(types[:, FULL_BLOCKS, :], 0).then_inc(s_pad, 1)
            pool.memset(ident[:, :], 0.0).then_inc(s_const, 1)
            pool.memset(own_j[:, :], 1.0).then_inc(s_const, 1)
            for v in (onehot3[:, :, :, :], bias_parts[:, :]):
                pool.memset(v, 0).then_inc(s_pad, 1)
            pool.wait_ge(s_const, 2)
            pool.affine_select(out=ident[:, :], in_=ident[:, :], compare_op=ALU.not_equal, fill=1.0,
                               base=0, pattern=[[-1, P]], channel_multiplier=1).then_inc(s_const, 1)
            pool.affine_select(out=own_j[:, :], in_=own_j[:, :], compare_op=ALU.is_ge, fill=0.0,
                               base=0, pattern=[[-T, BJ]], channel_multiplier=1).then_inc(s_const, 1)
            pool.wait_ge(s_const, 4)
            pool.affine_select(out=own_j[:, :], in_=own_j[:, :], compare_op=ALU.is_ge, fill=0.0,
                               base=T - 1, pattern=[[T, BJ]], channel_multiplier=-1).then_inc(s_const, 1)
            pool.memset(ones[:, :], 1.0).then_inc(s_const, 1)
            pool.iota(lane_base[:, :], [[0, 1]], base=-1, channel_multiplier=LANE_EDGES).then_inc(s_const, 1)
            for buf in (dI, nI, pI):
                pool.memset(buf, PAD_DST).then_inc(s_pad, 1)

            full = edge_attr[0:FULL_LANES * LANE_EDGES, :].rearrange("(p j) d -> p j d", j=LANE_EDGES)
            CHUNK_STEPS = T * (1 + ED.bit_length() - 1)

            def load_attr(c):
                lo, hi = c * ATTR_CHUNK, (c + 1) * ATTR_CHUNK
                if c == 0:
                    pool.wait_ge(s_idx, 1)
                    pool.wait_ge(s_setC, 2)
                    pool.memset(attr_c, 0.0).then_inc(s_score, 1)
                pool.wait_ge(s_score, 1 + CHUNK_STEPS * c)
                pool.dma_start(attr_c[0:112], full[0:112, lo:hi, :]).then_inc(s_attr, 16)
                pool.dma_start(attr_c[112:FULL_LANES], full[112:FULL_LANES, lo:hi, :]).then_inc(s_attr, 16)
                n = min(hi, LAST_LANE) - lo
                if n > 0:
                    e = FULL_LANES * LANE_EDGES + lo
                    pool.dma_start(attr_c[FULL_LANES:P, 0:n, :],
                                   edge_attr[e:e + n, :].rearrange("(a j) d -> a j d", a=1)).then_inc(s_attr, 16)

            def edge_scores(c):
                lo, hi = c * ATTR_CHUNK, (c + 1) * ATTR_CHUNK
                loads = sum(3 if LAST_LANE > q * ATTR_CHUNK else 2 for q in range(c + 1))
                pool.wait_ge(s_attr, 16 * loads)
                done = 1 + CHUNK_STEPS * c
                for t in range(T):
                    pool.tensor_tensor(attr_prod, attr_c, g_edge[:, t, :].unsqueeze(1)
                                       .to_broadcast([P, ATTR_CHUNK, ED]), ALU.mult).then_inc(s_score, 1)
                    done += 1
                    pool.wait_ge(s_score, done)
                    half = ED // 2
                    while half:
                        into = attr_prod[:, :, 0:half] if half > 1 else edge_score[:, lo:hi, t:t + 1]
                        pool.tensor_tensor(into, attr_prod[:, :, 0:half], attr_prod[:, :, half:2 * half],
                                           ALU.add).then_inc(s_score, 1)
                        done += 1
                        pool.wait_ge(s_score, done)
                        half //= 2

            def gather(idx, j, into, table, done):
                pool.indirect_dma_start(out=into, out_offset=None, in_=table, in_offset=bass.IndirectOffsetOnAxis(
                    ap=idx[:, j:j + 1], axis=0)).then_inc(done, 16)

            def gather_src(n, g, slot):
                for u in range(U):
                    gather(src_idx, g * U + u, xs_ring[:, slot, u * C:(u + 1) * C], x, s_gx[n % SLOTS])

            def src_landed(n):
                pool.wait_ge(s_gx[n % SLOTS], 16 * U * (n // SLOTS + 1))

            def gather_rows(g):
                if g >= SLOTS:
                    pool.wait_ge(e_z, g - SLOTS + 1)
                for u in range(U):
                    gather(row_idx, g * U + u, rows[:, g % SLOTS, u, :], node_rows, s_gr[g % SLOTS])

            def scatter_out(g):
                pool.wait_ge(e_norm, g + 1)
                for u in range(U):
                    j = g * U + u
                    pool.indirect_dma_start(
                        out=out, out_offset=bass.IndirectOffsetOnAxis(ap=out_idx[:, j:j + 1], axis=0),
                        in_=z[:, g % SLOTS, u, :], in_offset=None,
                        bounds_check=N - 1, oob_is_err=False).then_inc(s_sc[g % SLOTS], 16)

            pool.wait_ge(s_src, 48)
            def store_later(c):
                pool.wait_ge(s_later, 16 * c)
                pool.dma_start(later_rows[:, c * SLOTS * U:(c + 1) * SLOTS * U, :].rearrange("p n c -> p (n c)"),
                               xs_ring[:, c * SLOTS % RING:c * SLOTS % RING + SLOTS, :]
                               .rearrange("p g n -> p (g n)")).then_inc(s_later, 16)

            for n in range(LATER):
                gather_src(n, RING + DIRECT + n, n % RING)
                if n >= 3:
                    src_landed(n - 3)
                if n % SLOTS == 2 and n > SLOTS:
                    store_later(n // SLOTS - 1)
                if n % 6 == 5:
                    load_attr(n // 6)
                if n % 6 == 1 and n > 6:
                    edge_scores(n // 6 - 1)
            for n in range(3):
                src_landed(LATER - 3 + n)
            store_later(LATER // SLOTS - 1)
            edge_scores(3)
            for g in range(RING):
                if g == (LATER - SLOTS) % RING:
                    pool.wait_ge(s_later, 16 * (LATER // SLOTS))
                gather_src(LATER + g, g, g)
                if g >= 3:
                    src_landed(LATER + g - 3)
                    pool.sem_inc(s_xs, 1)
            for g in range(RING - 3, RING):
                src_landed(LATER + g)
                pool.sem_inc(s_xs, 1)
            for k in range(SLOTS):
                pool.wait_ge(s_row_out[k], 16 * ((BLOCKS - 1 - k) // SLOTS + 1))
            pool.wait_ge(s_idx, 1)
            for g in range(GROUPS + LAG):
                if g < SLOTS:
                    pool.wait_ge(s_bsel_used, 2 * (BLOCKS - (BLOCKS - 1 - g) % SLOTS))
                if g < GROUPS:
                    gather_rows(g)
                if g == SLOTS - 1:
                    for d in range(DIRECT):
                        pool.wait_ge(s_staged, d + 1)
                        gather_src(LATER + RING + d, RING + d, d)
                if g == SLOTS:
                    for d in range(DIRECT):
                        src_landed(LATER + RING + d)
                        pool.sem_inc(s_xs, 1)
                if g == LAG:
                    for k in range(SLOTS):
                        pool.wait_ge(s_out[k], 16 * ((BLOCKS - 1 - k) // SLOTS + 1))
                if g == GROUPS + LAG - 1:
                    pool.wait_ge(e_z, GROUPS)
                    gather(row_idx, 0, rows[:, 0, 0, :], node_rows, f_rows)
                    for q in range(2):
                        pool.wait_ge(s_keep[q], 16 * (GROUPS // 2))
                    gather(head_idx, 0, head_acc[:, :], acc_rows, f_head)
                if g >= LAG:
                    scatter_out(g - LAG)
            for k in range(SLOTS):
                pool.wait_ge(s_sc[k], 16 * U * (GROUPS // SLOTS))
            pool.wait_ge(f_act, 5)
            pool.indirect_dma_start(
                out=out, out_offset=bass.IndirectOffsetOnAxis(ap=fix_idx[:, 0:1], axis=0),
                in_=z[:, 0, 0, :], in_offset=None, bounds_check=N - 1, oob_is_err=False).then_inc(f_out, 16)
            pool.wait_ge(f_out, 16)

        @block.tensor
        def _(pe):
            def transpose(o, i, n, eye=ident):
                return nc.tensor.transpose(o, i, eye[0:n, 0:n])

            pe.wait_ge(s_onehots, 1)

            def size(b):
                return P if not isinstance(b, int) or b < FULL_BLOCKS else TAIL_P

            def node_types(b, k):
                p = size(b)
                pe.wait_ge(s_ohT, b)
                pe.wait_ge(s_rep, b + 1)
                transpose(ps_o[0:T * REP, 0:p], onehot3[0:p, k % 2, :, :].rearrange("p r n -> p (r n)"), p,
                          ident_b).then_inc(s_ohT_ps, 1)

            def node_sums(b, i, k):
                p = size(b)
                pe.wait_ge(s_row_in[k], 16 * (i + 1))
                pe.wait_ge(s_ohT, b + 1)
                for h in range(2):
                    pe.wait_ge(s_bsel_used, back(2 * b, 3 - h))
                    bank = banks[2 * (k % 2) + h][0:p, :]
                    nc.tensor.matmul(bank, lhsT=onehotT[:, k % 2, 0:p],
                                     rhs=bias_parts[:, h * 4 * C:(h + 1) * 4 * C], start=True, stop=False)
                    nc.tensor.matmul(bank.rearrange("p (j c) -> p j c", c=C), lhsT=ident[0:p, 0:p],
                                     rhs=rows[0:p, k, 4 * h:4 * h + 4, 0:C], start=False, stop=True)\
                        .then_inc(s_bsel, 1)

            def node_step(b, i, k):
                node_sums(b, i, k)
                if not isinstance(b, int) or b + 1 < BLOCKS:
                    node_types(b + 1, (k + 1) % SLOTS)

            node_types(0, 0)
            for b in range(SLOTS):
                node_step(b, 0, b)
                if b == 1:
                    pe.wait_ge(s_const, 6)
                    pe.wait_ge(s_par, 16 * PAR_LOADS)
                    for t in range(T):
                        transpose(ps_x[0][:, t * C:(t + 1) * C], W3[:, t, :], P)
                    for t in range(T):
                        last = transpose(ps_x[1][:, t * ED:(t + 1) * ED], We3[:, t, :], ED)
                    last.then_inc(s_setT, 1)
                if b == 3:
                    pe.wait_ge(s_setC, 1)
                    for t in range(T):
                        nc.tensor.matmul(ps_a[:, t:t + 1], lhsT=WT[:, t, :], rhs=a_src[:, t:t + 1],
                                         start=True, stop=True)
                        nc.tensor.matmul(ps_a[:, T + t:T + t + 1], lhsT=WT[:, t, :], rhs=a_dst[:, t:t + 1],
                                         start=True, stop=True)
                        last = nc.tensor.matmul(ps_a[:, 64 + t * ED:64 + (t + 1) * ED], lhsT=a_edge_bc[:, t, :],
                                                rhs=WeT[:, t, :], start=True, stop=True)
                    last.then_inc(s_setT, 1)
            with pe.Fori(1, BLOCK_LOOPS) as i:
                for k in range(SLOTS):
                    node_step(SLOTS * i + k, i, k)
            def source_transposed(g, k):
                pe.wait_ge(s_staged, g + 1)
                for h, (lo, hi) in enumerate(((0, 4), (4, U))):
                    pe.wait_ge(e_accT, back(2 * g, 3 - h))
                    pe.wait_ge(e_xdT, back(2 * g, 1 - h))
                    for u in range(lo, hi):
                        last = transpose(ps_x[h][:, (u - lo) * P:(u - lo + 1) * P], xst[:, k % 2, u, :], P)
                    last.then_inc(e_xT_ps, 1)

            def source_scores(g, k):
                pe.wait_ge(e_xT, 2 * g + 2)
                pe.wait_ge(e_al_used, g)
                for u in range(U):
                    nc.tensor.matmul(ps_a[:, u * T:(u + 1) * T], lhsT=xT[:, k % 2, u * P:(u + 1) * P],
                                     rhs=V_src[:, :], start=u == 0, stop=False)

            pe.wait_ge(s_setC, 2)
            source_transposed(0, 0)
            source_scores(0, 0)
            for b in range(SLOTS * BLOCK_LOOPS, BLOCKS):
                node_step(b, b // SLOTS, b % SLOTS)

            pe.wait_ge(s_ohT, BLOCKS)
            pe.wait_ge(s_bsel_used, 2 * BLOCKS)

            def dst_transposed(g, i, k):
                pe.wait_ge(s_gr[k], 16 * U * (i + 1))
                for h, (lo, hi) in enumerate(((0, 4), (4, U))):
                    pe.wait_ge(e_xT, 2 * g + 1 + h)
                    for u in range(lo, hi):
                        last = transpose(ps_x[h][:, (u - lo) * P:(u - lo + 1) * P], rows[:, k, u, 0:C], P)
                    last.then_inc(e_xdT_ps, 1)

            def dst_scores(g):
                pe.wait_ge(e_xdT, 2 * g + 2)
                for u in range(U):
                    last = nc.tensor.matmul(ps_a[:, u * T:(u + 1) * T], lhsT=xdT[:, u * P:(u + 1) * P],
                                            rhs=V_dst[:, :], start=False, stop=u == U - 1)
                last.then_inc(e_al, 1)

            def types_transposed(g, k):
                pe.wait_ge(e_rep, g + 1)
                pe.wait_ge(e_ohT, g)
                transpose(ps_o[0:T * REP, 0:P], onehot3[:, k % 2, :, :].rearrange("p r n -> p (r n)"), P, ident_b)\
                    .then_inc(e_ohT_ps, 1)

            def sums_transposed(g, k):
                q = k % 2
                for h, (lo, hi) in enumerate(((0, 4), (4, U))):
                    pe.wait_ge(e_xdT, 2 * g + 3 + h if not isinstance(g, int) else min(2 * g + 3 + h, 2 * GROUPS))
                    pe.wait_ge(e_acc, U * g + hi)
                    for u in range(lo, hi):
                        last = transpose(ps_x[h][:, (u - lo) * P:(u - lo + 1) * P], acc[:, q, u, :], P)
                    last.then_inc(e_accT_ps, 1)

            def apply_w(g, k, tiles):
                q = k % 2
                for u in tiles:
                    pe.wait_ge(e_accT, 2 * g + (1 if u < 4 else 2))
                    if u >= 4:
                        pe.wait_ge(e_w_used, U * g + u - 3)
                    elif u < 2:
                        pe.wait_ge(e_w_used, back(U * g, 2 - u))
                    else:
                        pe.wait_ge(e_bsel_used, 2 * g + u - 1)
                    nc.tensor.matmul(banks[u % 4][:, 0:T * C], lhsT=accT[:, q, u * P:(u + 1) * P],
                                     rhs=W3[:, :, :].rearrange("p t c -> p (t c)"), start=True, stop=True)\
                        .then_inc(e_w, 1)

            def biases(g, k):
                pe.wait_ge(e_ohT, g + 1)
                pe.wait_ge(e_w_used, U * g)
                for h, (lo, hi) in enumerate(((0, 4), (4, U))):
                    nc.tensor.matmul(ps_b[h][:, 0:(hi - lo) * C], lhsT=onehotT[:, k % 2, :],
                                     rhs=bias_parts[:, lo * C:hi * C], start=True, stop=True).then_inc(e_bsel, 1)

            def edge_step(g, i, k):
                known = isinstance(g, int)
                if not known or g + 1 < GROUPS:
                    dst_scores(g + 1)
                if not known or g > 0:
                    apply_w(g - 1, (k + 3) % SLOTS, (4, 5, 6))
                if not known or g < GROUPS:
                    sums_transposed(g, k)
                    biases(g, k)
                    apply_w(g, k, (0, 1))
                    if not known or g + 2 < GROUPS:
                        source_transposed(g + 2, (k + 2) % SLOTS)
                    apply_w(g, k, (2, 3))
                    if not known or g + 1 < GROUPS:
                        types_transposed(g + 1, (k + 1) % SLOTS)
                    if not known or g + 2 < GROUPS:
                        dst_transposed(g + 2, i + (1 if k >= 2 else 0), (k + 2) % SLOTS)
                        source_scores(g + 2, (k + 2) % SLOTS)

            dst_transposed(0, 0, 0)
            dst_scores(0)
            source_transposed(1, 1)
            source_scores(1, 1)
            types_transposed(0, 0)
            dst_transposed(1, 0, 1)
            for g in range(SLOTS):
                edge_step(g, 0, g)
            with pe.Fori(1, GROUPS // SLOTS - 1) as i:
                for k in range(SLOTS):
                    edge_step(SLOTS * i + k, i, k)
            for g in range(GROUPS - SLOTS, GROUPS + 1):
                edge_step(g, g // SLOTS, g % SLOTS)

            pe.wait_ge(f_dve, 1)
            for c in range(5):
                last = transpose(ps_x[c // 4][0:1, (c % 4) * P:(c % 4 + 1) * P], cols[:, c:c + 1], P)
            last.then_inc(f_pe, 1)
            pe.wait_ge(f_dve, 3)
            nc.tensor.matmul(ps_b[0][:, :], lhsT=ones[0:1, :], rhs=xT[0:1, 1, 0:4 * P], start=True, stop=True)
            nc.tensor.matmul(ps_b[1][:, 0:1], lhsT=xT[0:1, 1, 4 * P:5 * P], rhs=ones[0:1, 0:1],
                             start=True, stop=True).then_inc(f_pe, 1)
            transpose(ps_w[0][:, 0:P], acc[:, (GROUPS - 1) % 2, U - 1, :], P)
            pe.wait_ge(f_head, 16)
            transpose(ps_w[0][:, P:2 * P], head_acc[:, :], P).then_inc(f_pe, 1)
            pe.wait_ge(f_rows, 16)
            pe.wait_ge(f_act, 2)
            transpose(ps_o[0:T * REP, 0:P], onehot3[:, 0, :, :].rearrange("p r n -> p (r n)"), P, ident_b)\
                .then_inc(f_pe, 1)
            pe.wait_ge(f_dve, 4)
            nc.tensor.matmul(ps_w[1][:, 0:T * C], lhsT=accT[:, 0, 0:P], rhs=W3[:, :, :].rearrange("p t c -> p (t c)"),
                             start=True, stop=True).then_inc(f_pe, 1)
            pe.wait_ge(f_act, 3)
            nc.tensor.matmul(ps_a[:, 0:C], lhsT=onehotT[:, 0, :], rhs=bias_parts[:, 0:C],
                             start=True, stop=True).then_inc(f_pe, 1)

        @block.scalar
        def _(act):
            def copy(o, i):
                return nc.scalar.activation(o, i, ACT.Copy)

            def normalise(zz, q, first, n, p, done):
                for j in range(n):
                    last = nc.scalar.activation(zz[0:p, j, :], zz[0:p, j, :], ACT.Identity,
                                                bias=nbias[0:p, q, first + j:first + j + 1],
                                                scale=rstd[0:p, q, first + j:first + j + 1])
                last.then_inc(done, 1)

            act.wait_ge(s_onehots, 1)

            def size(b):
                return P if not isinstance(b, int) or b < FULL_BLOCKS else TAIL_P

            def types_copied(b, k):
                p = size(b)
                act.wait_ge(s_ohT_ps, back(b, 1))
                act.wait_ge(s_row_oh, b + 1)
                copy(onehot3[0:p, k % 2, :, 0:BJ * T].rearrange("p r (j t) -> p r j t", t=T),
                     rows[0:p, k, :, C:ROW].unsqueeze(1).to_broadcast([p, 3, BJ, T])).then_inc(s_rep, 1)

            def types_out(b, k):
                p = size(b)
                act.wait_ge(s_ohT_ps, b + 1)
                act.wait_ge(s_bsel, back(2 * b, 2))
                copy(onehotT[:, k % 2, 0:p], ps_o[0:T * REP, 0:p]).then_inc(s_ohT, 1)

            def rows_types(b, i, k):
                act.wait_ge(s_row_in[k], 16 * (i + 1))
                copy(rows[0:size(b), k, :, C:ROW], onehot_all[0:size(b), b, :]
                     .rearrange("p (j t) -> p j t", t=T)).then_inc(s_row_oh, 1)

            def deviations(b, k):
                act.wait_ge(s_var, b + 1)
                nc.scalar.activation(std[:, k % 2, 0:BJ], st[:, k % 2, 4, 0:BJ], ACT.Sqrt, bias=eps[:, :])\
                    .then_inc(s_std, 1)

            def layer_norm(b, k):
                act.wait_ge(s_norm_par, b + 1)
                normalise(z[:, k], k % 2, 0, BJ, size(b), s_norm)

            def node_step(b, i, k):
                known = isinstance(b, int)
                if not known or b > 0:
                    deviations(b - 1, (k + 3) % SLOTS)
                if not known or b + 1 < BLOCKS:
                    types_out(b + 1, (k + 1) % SLOTS)
                if not known or b + 2 < BLOCKS:
                    rows_types(b + 2, i + (1 if k >= 2 else 0), (k + 2) % SLOTS)
                    types_copied(b + 2, (k + 2) % SLOTS)
                if not known or b > 0:
                    layer_norm(b - 1, (k + 3) % SLOTS)

            rows_types(0, 0, 0)
            rows_types(1, 0, 1)
            types_copied(0, 0)
            types_copied(1, 1)
            types_out(0, 0)
            for b in range(SLOTS):
                node_step(b, 0, b)
            with act.Fori(1, BLOCK_LOOPS) as i:
                for k in range(SLOTS):
                    node_step(SLOTS * i + k, i, k)
            act.wait_ge(s_idx, 1)

            def stage(g, slot, k):
                act.wait_ge(s_xs, g + 1)
                act.wait_ge(e_xT_ps, back(2 * g, 2))
                act.wait_ge(e_px, back(U * g, U))
                copy(xst[:, k % 2, :, :].rearrange("p u c -> p (u c)"), xs_ring[:, slot, :]).then_inc(s_staged, 1)

            def source_out(g, k):
                act.wait_ge(e_al, back(g, 1))
                for h, (lo, hi) in enumerate(((0, 4), (4, U))):
                    act.wait_ge(e_xT_ps, 2 * g + h + 1)
                    copy(xT[:, k % 2, lo * P:hi * P], ps_x[h][:, 0:(hi - lo) * P]).then_inc(e_xT, 1)

            stage(0, 0, 0)
            stage(1, 1, 1)
            source_out(0, 0)
            for b in range(SLOTS * BLOCK_LOOPS, BLOCKS + 1):
                node_step(b, b // SLOTS, b % SLOTS)

            act.wait_ge(s_bsel, 2 * BLOCKS)

            def types_copied(g, i, k):
                act.wait_ge(s_gr[k], 16 * U * (i + 1))
                copy(onehot3[:, k % 2, :, 0:U * T].rearrange("p r (j t) -> p r j t", t=T),
                     rows[:, k, 0:U, C:ROW].unsqueeze(1).to_broadcast([P, 3, U, T])).then_inc(e_rep, 1)

            def types_out(g, k):
                act.wait_ge(e_ohT_ps, g + 1)
                act.wait_ge(e_bsel, back(2 * g, 2))
                copy(onehotT[:, k % 2, :], ps_o[0:T * REP, 0:P]).then_inc(e_ohT, 1)

            def dst_out(g):
                act.wait_ge(e_al, g)
                for h, (lo, hi) in enumerate(((0, 4), (4, U))):
                    act.wait_ge(e_xdT_ps, 2 * g + h + 1)
                    copy(xdT[:, lo * P:hi * P], ps_x[h][:, 0:(hi - lo) * P]).then_inc(e_xdT, 1)

            def acc_out(g, k, h):
                lo, hi = (0, 4) if h == 0 else (4, U)
                act.wait_ge(e_accT_ps, 2 * g + h + 1)
                if h == 0:
                    act.wait_ge(e_w, back(U * g, U))
                copy(accT[:, k % 2, lo * P:hi * P], ps_x[h][:, 0:(hi - lo) * P]).then_inc(e_accT, 1)

            def weights(g, k):
                q = k % 2
                act.wait_ge(e_expo, g + 1)
                nc.scalar.activation(fp[:, q, :, :], expo[:, q, :, :], ACT.Exp).then_inc(e_exp, 1)

            def weighted(g, k):
                q = k % 2
                act.wait_ge(e_exp, g + 1)
                act.wait_ge(e_acc, U * g)
                for u in range(U):
                    nc.scalar.activation(px[:, u, :], xst[:, q, u, :], ACT.Copy,
                                         scale=fp[:, q, 1, u:u + 1]).then_inc(e_px, 1)

            def edge_std(g, k):
                act.wait_ge(e_var, g + 1)
                nc.scalar.activation(std[:, k % 2, 0:U], st[:, k % 2, 4, 0:U], ACT.Sqrt, bias=eps[:, :])\
                    .then_inc(e_std, 1)

            def edge_norm(g, k):
                act.wait_ge(e_norm_par, g + 1)
                normalise(z[:, k], k % 2, 0, U, P, e_norm)

            def edge_step(g, i, k):
                known = isinstance(g, int)
                if not known or g >= 2:
                    edge_std(g - 2, (k + 2) % SLOTS)
                if not known or g + 2 < GROUPS:
                    stage(g + 2, (g + 2) % RING, (k + 2) % SLOTS)
                if not known or g < GROUPS:
                    acc_out(g, k, 0)
                if not known or g >= 2:
                    edge_norm(g - 2, (k + 2) % SLOTS)
                if not known or g < GROUPS:
                    acc_out(g, k, 1)
                if not known or g + 2 < GROUPS:
                    source_out(g + 2, (k + 2) % SLOTS)
                if not known or g + 1 < GROUPS:
                    types_copied(g + 1, i + (1 if k == SLOTS - 1 else 0), (k + 1) % SLOTS)
                    weights(g + 1, (k + 1) % SLOTS)
                if not known or g + 2 < GROUPS:
                    dst_out(g + 2)
                if not known or g + 1 < GROUPS:
                    weighted(g + 1, (k + 1) % SLOTS)
                    types_out(g + 1, (k + 1) % SLOTS)

            dst_out(0)
            source_out(1, 1)
            types_copied(0, 0, 0)
            weights(0, 0)
            dst_out(1)
            weighted(0, 0)
            types_out(0, 0)
            for g in range(SLOTS):
                edge_step(g, 0, g)
            with act.Fori(1, GROUPS // SLOTS - 1) as i:
                for k in range(SLOTS):
                    edge_step(SLOTS * i + k, i, k)
            for g in range(GROUPS - SLOTS, GROUPS + 2):
                edge_step(g, g // SLOTS, g % SLOTS)

            act.wait_ge(f_dve, 2)
            nc.scalar.activation(xT[0:1, 1, 0:4 * P], xT[0:1, 0, 0:4 * P], ACT.Exp).then_inc(f_act, 1)
            act.wait_ge(f_rows, 16)
            copy(onehot3[:, 0, :, 0:T], rows[:, 0, 0:1, C:ROW].to_broadcast([P, 3, T])).then_inc(f_act, 1)
            act.wait_ge(f_pe, 4)
            copy(onehotT[:, 0, :], ps_o[0:T * REP, 0:P]).then_inc(f_act, 1)
            act.wait_ge(f_dve, 5)
            nc.scalar.activation(std[:, 0, 0:1], st[:, 0, 4, 0:1], ACT.Sqrt, bias=eps[:, :]).then_inc(f_act, 1)
            act.wait_ge(f_dve, 6)
            act.wait_ge(s_sc[0], 16 * U * (GROUPS // SLOTS))
            normalise(z[:, 0], 0, 0, 1, P, f_act)

        @block.vector
        def _(dve):
            tt = nc.vector.tensor_tensor
            ts = nc.vector.tensor_scalar
            stt = nc.vector.scalar_tensor_tensor

            class Order:

                def __init__(self, sem, base, total=None):
                    self.sem, self.base, self.total, self.n = sem, base, total, 0

                def done(self, instruction):
                    instruction.then_inc(self.sem, 1)
                    self.n += 1
                    return self.base + self.n

                def wait(self):
                    dve.wait_ge(self.sem, self.base + self.n)

                def link(self, instruction):
                    self.done(instruction)
                    self.wait()

                def end(self):
                    assert self.total in (None, self.n), self.n

            o = Order(s_dve_setup, 0)
            for v, value in ((eps[:, :], EPS), (M_all[:, 0:1], -BIG), (S_all[:, 0:1], 0.0),
                             (stats[:, :, :, :], 0.0)):
                o.done(nc.vector.memset(v, value))

            dve.wait_ge(s_const, 7)
            o.link(nc.vector.tensor_copy(ident_b[:, :], ident[:, :]))
            dve.wait_ge(s_bias, 16 * BIAS_LOADS)
            dve.wait_ge(s_pad, 4)
            for r in range(3):
                o.link(nc.vector.tensor_copy(bias_split[:, r, :], bias_rows[:, :]))
                if r < 2:
                    o.link(tt(bias_rows[:, :], bias_rows[:, :], bias_split[:, r, :], ALU.subtract))
                o.done(tt(bias_parts[r * REP:r * REP + BJ * T, :].rearrange("p (j c) -> p j c", c=C),
                          bias_split[:, r, :].unsqueeze(1).to_broadcast([BJ * T, BJ, C]),
                          own_j[:, :].unsqueeze(2).to_broadcast([BJ * T, BJ, C]), ALU.mult))
            o.wait()

            dve.wait_ge(s_types, 32)
            one = lambda t: onehot_all[:, :, :].rearrange("p b (j t) -> p b j t", t=T)[:, :, :, t]
            o.done(ts(one(0), types[:, :, :], 0.0, None, ALU.is_equal))
            o.done(ts(one(1), types[:, :, :], 1.0, None, ALU.is_equal))
            o.wait()
            o.link(tt(one(2), one(0), one(1), ALU.add))
            ts(one(2), one(2), -1.0, 1.0, ALU.mult, ALU.add).then_inc(s_onehots, 1)

            def transposed_parameters(o):
                dve.wait_ge(s_par, 16 * PAR_LOADS)
                for t in range(T):
                    o.done(ts(a_edge_bc[:, t, :], ones[:, :], a_edge[:, t:t + 1], None, ALU.mult))
                dve.wait_ge(s_setT, 1)
                o.done(nc.vector.tensor_copy(WT[:, :, :].rearrange("p t c -> p (t c)"), ps_x[0][:, 0:T * C]))
                o.wait()
                nc.vector.tensor_copy(WeT[:, :, :].rearrange("p t c -> p (t c)"), ps_x[1][:, 0:T * ED])\
                    .then_inc(s_setC, 1)

            def projections(o):
                dve.wait_ge(s_setT, 2)
                o.done(nc.vector.tensor_copy(V_src[:, :], ps_a[:, 0:T]))
                o.done(nc.vector.tensor_copy(V_dst[:, :], ps_a[:, T:2 * T]))
                o.wait()
                nc.vector.tensor_copy(g_edge[:, :, :].rearrange("p t c -> p (t c)"), ps_a[:, 64:64 + T * ED])\
                    .then_inc(s_setC, 1)

            last = LANE_EDGES - 1
            carries, inner, ends_here, fix = (cin[:, c:c + 1] for c in range(4))

            def edge_flags(o):
                dve.wait_ge(s_dst, 16 * 9)
                for f, i in ((dF, dI), (nF, nI), (pF, pI)):
                    o.done(nc.vector.tensor_copy(f, i))
                o.wait()
                o.done(ts(hd, dF, dF[:, 0:1], None, ALU.is_equal))
                o.done(tt(carries, pF[:, 0:1], dF[:, 0:1], ALU.is_equal))
                o.done(tt(restart[:, :], pF, dF, ALU.not_equal))
                o.wait()
                o.done(ts(restart[:, :], restart[:, :], -BIG, None, ALU.mult))
                o.done(tt(pF, nF, dF, ALU.not_equal))

            def head_flags(o):
                o.wait()
                o.done(nc.vector.memset(restart[:, 0:1], -BIG))
                o.done(tt(head_end[:, 0:last], hd[:, 0:last], pF[:, 0:last], ALU.mult))
                o.done(nc.vector.tensor_copy(head_end[:, last:], hd[:, last:]))
                o.done(nc.vector.tensor_reduce(rs[:, 0:1], hd, X_AXIS, ALU.add))
                o.done(tt(cols[:, 4:5], carries, hd[:, last:], ALU.mult))
                o.done(ts(nF, hd, carries, None, ALU.mult))
                o.done(ts(inner, pF[:, last:], -1.0, 1.0, ALU.mult, ALU.add))

            def edge_indices(o):
                o.wait()
                o.done(tt(head_idx[:, :], lane_base[:, :], rs[:, 0:1], ALU.add))
                o.done(ts(nF, nF, -1.0, 1.0, ALU.mult, ALU.add))
                o.done(tt(inner, inner, hd[:, last:], ALU.mult))
                o.wait()
                o.done(tt(nF, nF, pF, ALU.mult))
                o.done(ts(ends_here, inner, -1.0, 1.0, ALU.mult, ALU.add))
                o.wait()
                o.done(ts(nF, nF, -float(SKIP), float(SKIP), ALU.mult, ALU.add))
                o.done(tt(fix, ends_here, carries, ALU.mult))
                o.wait()
                o.done(tt(out_idx[:, :], nF, dF, ALU.add))
                o.done(ts(fix, fix, -float(SKIP), float(SKIP), ALU.mult, ALU.add))
                o.done(ts(row_idx[:, :], dF, float(N - 1), None, ALU.min))
                o.wait()
                o.link(tt(fix_idx[:, :], fix, dF[:, 0:1], ALU.add))
                dve.sem_inc(s_idx, 1)

            def block_statistics(o, zz, q, tiles, p):
                for j in tiles:
                    o.done(nc.vector.bn_stats(stats[0:p, q, j, :], zz[0:p, j, :]))

            def variances(o, q, n, done):
                o.wait()
                f = lambda c: stats[:, q, 0:n, c]
                v = lambda c: st[:, q, c, 0:n]
                o.done(tt(v(1), f(1), f(4), ALU.subtract))
                o.done(tt(v(0), f(1), f(4), ALU.add))
                o.done(tt(v(2), f(2), f(5), ALU.add))
                o.wait()
                o.link(stt(v(3), v(1), 0.25, v(1), ALU.mult, ALU.mult))
                stt(v(4), v(2), 1.0 / C, v(3), ALU.mult, ALU.add).then_inc(done, 1)

            def norm_scale(o, q, n):
                o.done(nc.vector.reciprocal(rstd[:, q, 0:n], std[:, q, 0:n]))

            def norm_bias(o, q, n, done):
                o.wait()
                stt(nbias[:, q, 0:n], st[:, q, 0, 0:n], -0.5, rstd[:, q, 0:n], ALU.mult, ALU.mult)\
                    .then_inc(done, 1)

            def node_step(b, i, k):
                known = isinstance(b, int)
                this, last = not known or b < BLOCKS, not known or b > 0
                p = P if not known or b < FULL_BLOCKS else TAIL_P
                q = k % 2
                scale_order = Order(s_node_np, b - 1, 1)
                order = Order(s_node_st, 12 * b, 12)

                def residual(h):
                    dve.wait_ge(s_bsel, 2 * b + h + 1)
                    stt(z[0:p, k, 4 * h:4 * h + 4, :],
                        banks[2 * q + h][0:p, :].rearrange("p (j c) -> p j c", c=C), 0.0,
                        rows[0:p, k, 4 * h:4 * h + 4, 0:C], ALU.max, ALU.add).then_inc(s_bsel_used, 1)

                if this:
                    dve.wait_ge(s_out[k], 16 * i)
                    dve.wait_ge(s_row_in[k], 16 * (i + 1))
                    residual(0)
                if last:
                    dve.wait_ge(s_std, b)
                    norm_scale(scale_order, 1 - q, BJ)
                if this:
                    residual(1)
                if last:
                    norm_bias(scale_order, 1 - q, BJ, s_norm_par)
                if this:
                    dve.wait_ge(s_bsel_used, 2 * b + 1)
                    block_statistics(order, z[:, k], q, range(4), p)
                    dve.wait_ge(s_bsel_used, 2 * b + 2)
                    block_statistics(order, z[:, k], q, range(4, BJ), p)
                    variances(order, q, BJ, s_var)
                    order.end()

            par, flags = Order(s_dve_par, 0), Order(s_dve_flags, 0)
            for b in range(2 * SLOTS):
                node_step(b, b // SLOTS, b % SLOTS)
                if b == 1:
                    transposed_parameters(par)
                if b == 2:
                    edge_flags(flags)
                if b == 3:
                    head_flags(flags)
                if b == 4:
                    projections(par)
                if b == 5:
                    edge_indices(flags)
            with dve.Fori(2, BLOCK_LOOPS) as i:
                for k in range(SLOTS):
                    node_step(SLOTS * i + k, i, k)
            for b in range(SLOTS * BLOCK_LOOPS, BLOCKS + 1):
                node_step(b, b // SLOTS, b % SLOTS)

            dve.wait_ge(s_norm, BLOCKS)
            dve.wait_ge(s_score, 61)
            for k in range(SLOTS):
                dve.wait_ge(s_out[k], 16 * ((BLOCKS - 1 - k) // SLOTS + 1))
            nc.vector.memset(acc[:, 1, U - 1, :], 0.0).then_inc(e_zero, 1)
            dve.wait_ge(e_zero, 1)

            def columns(t, g, n=U):
                return t[:, bass.ds(g * U, n)]

            def exponents(g, i, k, o, part):
                q = k % 2
                sc = score[:, q, 0:U]
                M_new = M_all[:, bass.ds(g * U + 1, U)]
                if part == 0:
                    dve.wait_ge(s_gr[k], 16 * U * (i + 1))
                    dve.wait_ge(e_al, g + 1)
                    tt(prod[:, q, 0:U, :], ps_a[:, 0:U * T].rearrange("p (j t) -> p j t", t=T),
                       edge_score[:, bass.ds(g * U, U), :], ALU.add).then_inc(e_al_used, 1)
                    return
                if part == 1:
                    dve.wait_ge(e_al_used, g + 1)
                    o.done(tt(prod[:, q, 0:U, :], prod[:, q, 0:U, :], rows[:, k, 0:U, C:ROW], ALU.mult))
                    return
                o.wait()
                if part == 2:
                    o.done(nc.vector.tensor_reduce(sc, prod[:, q, 0:U, :], X_AXIS, ALU.add))
                elif part == 3:
                    o.done(stt(sc, sc, 0.2, sc, ALU.mult, ALU.max))
                elif part == 4:
                    o.done(nc.vector.tensor_tensor_scan(M_new, columns(restart, g), sc, columns(M_all, g, 1),
                                                        ALU.add, ALU.max))
                elif part == 5:
                    o.done(tt(expo[:, q, 0, :], columns(M_all, g), columns(restart, g), ALU.add))
                elif part == 6:
                    o.done(tt(expo[:, q, 0, :], expo[:, q, 0, :], M_new, ALU.subtract))
                else:
                    tt(expo[:, q, 1, :], sc, M_new, ALU.subtract).then_inc(e_expo, 1)

            def state_sums(g, q):
                dve.wait_ge(e_exp, g + 1)
                nc.vector.tensor_tensor_scan(S_all[:, bass.ds(g * U + 1, U)], fp[:, q, 0, :], fp[:, q, 1, :],
                                             columns(S_all, g, 1), ALU.mult, ALU.add).then_inc(e_scan, 1)

            def add_source(g, q, u):
                before = acc[:, q, u - 1, :] if u else acc[:, 1 - q, U - 1, :]
                dve.wait_ge(e_px, U * g + u + 1)
                dve.wait_ge(e_acc, U * g + u)
                stt(acc[:, q, u, :], before, fp[:, q, 0, u:u + 1], px[:, u, :], ALU.mult, ALU.add)\
                    .then_inc(e_acc, 1)

            def divisors(g, k, o, part):
                q = k % 2
                if part == 0:
                    dve.wait_ge(e_scan, g + 1)
                    o.done(ts(rs[:, 0:U], S_all[:, bass.ds(g * U + 1, U)], TINY, None, ALU.add))
                elif part == 1:
                    o.wait()
                    o.done(nc.vector.reciprocal(rs[:, 0:U], rs[:, 0:U]))
                else:
                    o.wait()
                    o.done(tt(kk[:, q, :, :], rows[:, k, 0:U, C:ROW],
                              rs[:, 0:U].unsqueeze(2).to_broadcast([P, U, T]), ALU.mult))

            def residuals(g, k, h):
                lo, hi = (0, 4) if h == 0 else (4, U)
                dve.wait_ge(e_bsel, 2 * g + h + 1)
                tt(z[:, k, lo:hi, :], ps_b[h][:, 0:(hi - lo) * C].rearrange("p (j c) -> p j c", c=C),
                   rows[:, k, lo:hi, 0:C], ALU.add).then_inc(e_bsel_used, 1)

            def edge_step(g, i, k):
                known = isinstance(g, int)
                this, last = not known or g < GROUPS, not known or 0 < g <= GROUPS
                before, ahead = not known or g > 1, not known or g + 1 < GROUPS
                q, lk, nk = k % 2, (k + 3) % SLOTS, (k + 1) % SLOTS
                ni = i + (1 if k == SLOTS - 1 else 0)
                sums = Order(e_dve_b, 3 * g, 3)
                norm = Order(e_dve_n, g - 2, 1)
                outs = Order(e_dve_c, 25 * (g - 1), 25)
                expos = Order(e_dve_a, 6 * (g + 1), 6)

                if this:
                    state_sums(g, q)
                    dve.wait_ge(e_accT_ps, back(2 * g, 2))
                    dve.wait_ge(s_keep[q], 16 * (2 * i + k // 2))
                if last:
                    dve.wait_ge(e_bsel_used, 2 * g)
                added = {}
                rounds = [(tiles, t) for tiles in ((0, 1), (2, 3), (4, 5, 6)) for t in range(T)]
                for r, (tiles, t) in enumerate(rounds):
                    if this and 1 <= r <= U:
                        add_source(g, q, r - 1)
                    for u in tiles if last else ():
                        if t == 0:
                            dve.wait_ge(e_w, U * (g - 1) + u + 1)
                        else:
                            dve.wait_ge(e_dve_c, added[u])
                        ins = stt(z[:, lk, u, :], banks[u % 4][:, t * C:(t + 1) * C], kk[:, 1 - q, u, t:t + 1],
                                  z[:, lk, u, :], ALU.mult, ALU.add)
                        if t < T - 1:
                            added[u] = outs.done(ins)
                        else:
                            ins.then_inc(e_w_used, 1)
                    if this and 2 <= r < 5:
                        divisors(g, k, sums, r - 2)
                    if before and r == 5:
                        dve.wait_ge(e_std, g - 1)
                        norm_scale(norm, q, U)
                    if before and r == 6:
                        norm_bias(norm, q, U, e_norm_par)

                if ahead:
                    exponents(g + 1, ni, nk, expos, 0)
                if last:
                    dve.wait_ge(e_w_used, U * g)
                    stt(z[:, lk, 0:U, :], z[:, lk, 0:U, :], 0.0, rows[:, lk, 0:U, 0:C], ALU.max, ALU.add)\
                        .then_inc(e_z, 1)
                if ahead:
                    exponents(g + 1, ni, nk, expos, 1)
                if this:
                    dve.wait_ge(s_sc[k], 16 * U * i)
                    residuals(g, k, 0)
                if ahead:
                    exponents(g + 1, ni, nk, expos, 2)
                if this:
                    residuals(g, k, 1)
                if last:
                    dve.wait_ge(e_z, g)
                for u in range(U):
                    if ahead and u < 5:
                        exponents(g + 1, ni, nk, expos, 3 + u)
                    if last:
                        block_statistics(outs, z[:, lk], 1 - q, (u,), P)
                if last:
                    variances(outs, 1 - q, U, e_var)

            def lane_states(o):
                hM = px[:, 0:4, :].rearrange("p a c -> p (a c)")[:, 0:LANE_EDGES]
                for c, v in ((2, M_all), (3, S_all)):
                    o.link(tt(hM, v[:, 1:], head_end[:, :], ALU.mult))
                    o.link(nc.vector.tensor_reduce(cols[:, c:c + 1], hM, X_AXIS, ALU.add))
                    o.link(nc.vector.tensor_copy(cols[:, c - 2:c - 1], v[:, LANE_EDGES:]))
                dve.sem_inc(f_dve, 1)

            o = Order(e_dve_a, 0)
            for part in range(8):
                exponents(0, 0, 0, o, part)
            for g in range(SLOTS):
                edge_step(g, 0, g)
            with dve.Fori(1, GROUPS // SLOTS - 1) as i:
                for k in range(SLOTS):
                    edge_step(SLOTS * i + k, i, k)
            for g in range(GROUPS - SLOTS, GROUPS):
                edge_step(g, g // SLOTS, g % SLOTS)
            lane_states(Order(s_dve_states, 0))
            for g in range(GROUPS, GROUPS + 2):
                edge_step(g, g // SLOTS, g % SLOTS)

            o = Order(s_dve_last, 0)
            dve.wait_ge(e_z, GROUPS)
            dve.wait_ge(e_accT, 2 * GROUPS)
            row = xst[0:1, 0, :, :].rearrange("p a c -> p (a c)")
            tailM, tailS, headM, headS, through = (row[:, c * P:(c + 1) * P] for c in range(5))
            Kbuf, Sbuf = xT[0:1, 0, 512:512 + P + 1], xT[0:1, 0, 704:704 + P + 1]
            headMx, headSx = row[:, 5 * P:6 * P], row[:, 6 * P:7 * P]
            factor = lambda j: xT[0:1, 0, j * P:(j + 1) * P]
            expd = lambda j: xT[0:1, 1, j * P:(j + 1) * P]
            dve.wait_ge(f_pe, 1)
            o.done(nc.vector.tensor_copy(row[:, 0:4 * P], ps_x[0][0:1, :]))
            o.done(ts(through, ps_x[1][0:1, 0:P], -1.0, BIG, ALU.add, ALU.mult))
            o.done(nc.vector.memset(Kbuf[:, 0:1], -BIG))
            o.done(nc.vector.memset(Sbuf[:, 0:1], 0.0))
            o.wait()
            o.link(nc.vector.tensor_tensor_scan(Kbuf[:, 1:], through, tailM, -BIG, ALU.add, ALU.max))
            o.link(tt(factor(0), Kbuf[:, 0:P], through, ALU.add))
            o.link(tt(factor(0), factor(0), Kbuf[:, 1:], ALU.subtract))
            o.link(tt(factor(1), tailM, Kbuf[:, 1:], ALU.subtract))
            o.link(tt(headMx, Kbuf[:, 0:P], headM, ALU.max))
            o.link(tt(factor(2), Kbuf[:, 0:P], headMx, ALU.subtract))
            o.link(tt(factor(3), headM, headMx, ALU.subtract))
            dve.sem_inc(f_dve, 1)
            dve.wait_ge(f_act, 1)
            o.link(tt(tailS, tailS, expd(1), ALU.mult))
            o.link(nc.vector.tensor_tensor_scan(Sbuf[:, 1:], expd(0), tailS, 0.0, ALU.mult, ALU.add))
            o.link(tt(headSx, Sbuf[:, 0:P], expd(2), ALU.mult))
            o.link(tt(headS, headS, expd(3), ALU.mult))
            o.link(tt(headS, headS, headSx, ALU.add))
            o.link(ts(expd(4), headS, TINY, None, ALU.add))
            dve.sem_inc(f_dve, 1)

            dve.wait_ge(f_pe, 2)
            bc = lambda j: xT[:, 0, j * P:(j + 1) * P]
            carry = px[:, 0:2, :].rearrange("p a c -> p (a c)")[:, 0:P + 1]
            whole = accT[:, 0, 0:P]
            o.done(nc.vector.tensor_copy(xT[:, 0, 0:4 * P], ps_b[0][:, :]))
            o.done(nc.vector.reciprocal(rs[:, 0:1], ps_b[1][:, 0:1]))
            o.done(nc.vector.memset(carry[:, 0:1], 0.0))
            o.wait()
            dve.wait_ge(f_pe, 3)
            o.link(tt(bc(1), ps_w[0][:, 0:P], bc(1), ALU.mult))
            o.link(nc.vector.tensor_tensor_scan(carry[:, 1:], bc(0), bc(1), 0.0, ALU.mult, ALU.add))
            o.link(tt(bc(3), ps_w[0][:, P:2 * P], bc(3), ALU.mult))
            o.link(tt(bc(2), carry[:, 0:P], bc(2), ALU.mult))
            o.link(tt(whole, bc(2), bc(3), ALU.add))
            dve.sem_inc(f_dve, 1)

            dve.wait_ge(f_rows, 16)
            o.link(ts(kk[:, 0, 0, :], rows[:, 0, 0, C:ROW], rs[:, 0:1], None, ALU.mult))
            dve.wait_ge(f_pe, 6)
            dve.wait_ge(s_sc[0], 16 * U * (GROUPS // SLOTS))
            o.link(tt(z[:, 0, 0, :], ps_a[:, 0:C], rows[:, 0, 0, 0:C], ALU.add))
            for t in range(T):
                o.link(stt(z[:, 0, 0, :], ps_w[1][:, t * C:(t + 1) * C], kk[:, 0, 0, t:t + 1], z[:, 0, 0, :],
                           ALU.mult, ALU.add))
            o.link(stt(z[:, 0, 0, :], z[:, 0, 0, :], 0.0, rows[:, 0, 0, 0:C], ALU.max, ALU.add))
            block_statistics(o, z[:, 0], 0, (0,), P)
            variances(o, 0, 1, f_dve)
            dve.wait_ge(f_act, 4)
            norm_scale(o, 0, 1)
            norm_bias(o, 0, 1, f_dve)


_PARAMS = ("W", "as", "ad", "We", "ae", "b")


def kernel(**inputs):
    import numpy as np
    import concourse.bacc as bacc
    from concourse.bass_utils import run_bass_kernel_spmd

    nc = bacc.Bacc("TRN2", target_bir_lowering=False, num_devices=1)
    arrays = {}

    def given(name):
        a = np.ascontiguousarray(inputs[name])
        arrays[f"in_{name}_dram"] = a
        return nc.dram_tensor(f"in_{name}_dram", a.shape, mybir.dt.from_np(a.dtype), kind="ExternalInput").ap()

    graph = [given(name) for name in ("x", "src", "dst", "edge_attr_16", "node_type_3")]
    convs = [[given(f"L0_gnn_{p}{c}") for p in _PARAMS] for c in "vri"]
    shape = inputs["x"].shape
    out = nc.dram_tensor("out_0_dram", shape, mybir.dt.float32, kind="ExternalOutput").ap()
    gat_kernel(nc, *graph, convs, out)
    r = run_bass_kernel_spmd(nc, [arrays], core_ids=[0])
    return r.results[0]["out_0_dram"]
```
